# Optimizing a Trainium2 kernel written in Bass

```python
import numpy as np
import jax
import jax.numpy as jnp

def _softmax(x, axis=-1):
    return jax.nn.softmax(x, axis=axis)

def _gelu(x):
    return jax.nn.gelu(x, approximate=True)

def _silu(x):
    return jax.nn.silu(x)

def _sigmoid(x):
    return jax.nn.sigmoid(x)

def _layernorm(x, axis=-1, eps=1e-05):
    m = jnp.mean(x, axis=axis, keepdims=True)
    v = jnp.var(x, axis=axis, keepdims=True)
    return (x - m) / jnp.sqrt(v + eps)

def _scatter_add(tgt, idx, src, axis=0):
    return tgt.at[idx].add(src)

def _segment_sum(src, seg, n):
    return jax.ops.segment_sum(src, seg, n)
kernel_name = 'mk_conv_preact_d4_conv_nchw8_r2_9cd7cc'

def setup_inputs(seed: int=0):
    np.random.seed(seed)
    _w = jnp.asarray

    def _rec_inputs():
        import jax
        import jax.numpy as jnp
        _gk = jax.random.key(seed)
        x = 0.5001 + 0.2887 * jax.random.normal(jax.random.fold_in(_gk, 1), (16, 8, 256, 256), jnp.float32)
        return x
    x = _rec_inputs()

    def _L0_conv_setup():
        import jax, jax.numpy as jnp
        import numpy as np
        KERNEL = np.ones((3, 3), dtype=np.float32)
        BORDER_VAL = -2.0
        key = jax.random.key(seed)
        img = jax.random.uniform(key, (16, 8, 256, 256), dtype=jnp.float32)
        return {'img': img}
    _L0_conv_all = _L0_conv_setup()
    _L0_conv_in = {k: v for k, v in _L0_conv_all.items() if k in ()}
    del _L0_conv_all

    def _L1_conv_setup():
        import jax, jax.numpy as jnp
        import numpy as np
        from jax import lax
        R = 4
        C_IN = 8
        D_MODEL = C_IN * R * R
        D_STATE = 32
        D_INNER = 2 * D_MODEL
        D_CONV = 4
        DT_RANK = (D_MODEL + 15) // 16
        B, H, W = (16, 128, 128)

        def _pixel_unshuffle(x, r):
            b, c, h, w = x.shape
            x = x.reshape(b, c, h // r, r, w // r, r)
            x = x.transpose(0, 1, 3, 5, 2, 4)
            return x.reshape(b, c * r * r, h // r, w // r)

        def _pixel_shuffle(x, r):
            b, cr, h, w = x.shape
            c = cr // (r * r)
            x = x.reshape(b, c, r, r, h, w)
            x = x.transpose(0, 1, 4, 2, 5, 3)
            return x.reshape(b, c, h * r, w * r)

        def _layernorm(x, gamma, beta, eps=1e-05):
            mu = jnp.mean(x, axis=-1, keepdims=True)
            var = jnp.mean(jnp.square(x - mu), axis=-1, keepdims=True)
            return (x - mu) * lax.rsqrt(var + eps) * gamma + beta

        def _mamba(u, in_proj_w, conv_w, conv_b, x_proj_w, dt_proj_w, dt_proj_b, A_log, D, out_proj_w):
            xz = jnp.einsum('bld,ed->ble', u, in_proj_w)
            x_in, z = jnp.split(xz, 2, axis=-1)
            xc = x_in.transpose(0, 2, 1)
            xc = jnp.pad(xc, ((0, 0), (0, 0), (D_CONV - 1, 0)))
            xc = lax.conv_general_dilated(xc, conv_w, (1,), 'VALID', dimension_numbers=('NCH', 'OIH', 'NCH'), feature_group_count=D_INNER)
            xc = jax.nn.silu(xc.transpose(0, 2, 1) + conv_b)
            x_dbl = jnp.einsum('bld,ed->ble', xc, x_proj_w)
            dt, Bc, Cc = jnp.split(x_dbl, [DT_RANK, DT_RANK + D_STATE], axis=-1)
            dt = jax.nn.softplus(jnp.einsum('blr,dr->bld', dt, dt_proj_w) + dt_proj_b)
            A = -jnp.exp(A_log)

            def step(h, inputs):
                dt_t, x_t, B_t, C_t = inputs
                h = h * jnp.exp(dt_t[..., None] * A) + (dt_t * x_t)[..., None] * B_t[:, None, :]
                y = jnp.einsum('bds,bs->bd', h, C_t)
                return (h, y)
            h0 = jnp.zeros((u.shape[0], D_INNER, D_STATE), u.dtype)
            _, ys = lax.scan(step, h0, (dt.transpose(1, 0, 2), xc.transpose(1, 0, 2), Bc.transpose(1, 0, 2), Cc.transpose(1, 0, 2)))
            y = ys.transpose(1, 0, 2) + xc * D
            y = y * jax.nn.silu(z)
            return jnp.einsum('bld,ed->ble', y, out_proj_w)
        key = jax.random.key(seed)
        ks = jax.random.split(key, 12)

        def rn(k, shape, scale):
            return jax.random.normal(k, shape, dtype=jnp.float32) * scale
        inp = {'x': rn(ks[0], (B, C_IN, H, W), 1.0), 'ln_gamma': jnp.ones((D_MODEL,), jnp.float32), 'ln_beta': jnp.zeros((D_MODEL,), jnp.float32), 'in_proj_w': rn(ks[1], (2 * D_INNER, D_MODEL), D_MODEL ** (-0.5)), 'conv_w': rn(ks[2], (D_INNER, 1, D_CONV), D_CONV ** (-0.5)), 'conv_b': rn(ks[3], (D_INNER,), 0.02), 'x_proj_w': rn(ks[4], (DT_RANK + 2 * D_STATE, D_INNER), D_INNER ** (-0.5)), 'dt_proj_w': rn(ks[5], (D_INNER, DT_RANK), DT_RANK ** (-0.5)), 'dt_proj_b': rn(ks[6], (D_INNER,), 0.1), 'A_log': jnp.log(jnp.broadcast_to(jnp.arange(1, D_STATE + 1, dtype=jnp.float32), (D_INNER, D_STATE))), 'D': jnp.ones((D_INNER,), jnp.float32), 'out_proj_w': rn(ks[7], (D_MODEL, D_INNER), D_INNER ** (-0.5))}
        return inp
    _L1_conv_all = _L1_conv_setup()
    _L1_conv_in = {k: v for k, v in _L1_conv_all.items() if k in ('ln_gamma', 'ln_beta', 'in_proj_w', 'conv_w', 'conv_b', 'x_proj_w', 'dt_proj_w', 'dt_proj_b', 'A_log', 'D', 'out_proj_w')}
    del _L1_conv_all

    def _L2_conv_setup():
        import jax, jax.numpy as jnp
        import numpy as np
        import math
        B, C_IN, C_OUT = (32, 8, 8)
        H, W = (512, 512)
        KH, KW = (3, 3)
        STRIDE = 1
        PAD = 1
        key = jax.random.key(seed)
        k1, k2, k3 = jax.random.split(key, 3)
        stdv = math.sqrt(1.0 / (C_IN * KH * KW))
        x = jax.random.normal(k1, (B, C_IN, H, W), dtype=jnp.float32)
        weight = jax.random.uniform(k2, (C_OUT, C_IN, KH, KW), dtype=jnp.float32, minval=-stdv, maxval=stdv)
        bias = jax.random.uniform(k3, (C_OUT,), dtype=jnp.float32, minval=-stdv, maxval=stdv)
        return {'input': x, 'weight': weight, 'bias': bias}
    _L2_conv_all = _L2_conv_setup()
    _L2_conv_in = {k: v for k, v in _L2_conv_all.items() if k in ('weight', 'bias')}
    del _L2_conv_all

    def _L3_conv_setup():
        import jax, jax.numpy as jnp
        import numpy as np
        import math
        B, C_IN, C_OUT = (32, 8, 8)
        H, W = (512, 512)
        KH, KW = (3, 3)
        STRIDE = 1
        PAD = 1
        key = jax.random.key(seed)
        k1, k2, k3 = jax.random.split(key, 3)
        stdv = math.sqrt(1.0 / (C_IN * KH * KW))
        x = jax.random.normal(k1, (B, C_IN, H, W), dtype=jnp.float32)
        weight = jax.random.uniform(k2, (C_OUT, C_IN, KH, KW), dtype=jnp.float32, minval=-stdv, maxval=stdv)
        bias = jax.random.uniform(k3, (C_OUT,), dtype=jnp.float32, minval=-stdv, maxval=stdv)
        return {'input': x, 'weight': weight, 'bias': bias}
    _L3_conv_all = _L3_conv_setup()
    _L3_conv_in = {k: v for k, v in _L3_conv_all.items() if k in ('weight', 'bias')}
    del _L3_conv_all
    return {'x': x, 'L1_conv_ln_gamma': _L1_conv_in['ln_gamma'], 'L1_conv_ln_beta': _L1_conv_in['ln_beta'], 'L1_conv_in_proj_w': _L1_conv_in['in_proj_w'], 'L1_conv_conv_w': _L1_conv_in['conv_w'], 'L1_conv_conv_b': _L1_conv_in['conv_b'], 'L1_conv_x_proj_w': _L1_conv_in['x_proj_w'], 'L1_conv_dt_proj_w': _L1_conv_in['dt_proj_w'], 'L1_conv_dt_proj_b': _L1_conv_in['dt_proj_b'], 'L1_conv_A_log': _L1_conv_in['A_log'], 'L1_conv_D': _L1_conv_in['D'], 'L1_conv_out_proj_w': _L1_conv_in['out_proj_w'], 'L2_conv_weight': _L2_conv_in['weight'], 'L2_conv_bias': _L2_conv_in['bias'], 'L3_conv_weight': _L3_conv_in['weight'], 'L3_conv_bias': _L3_conv_in['bias']}

def reference(x, L1_conv_ln_gamma, L1_conv_ln_beta, L1_conv_in_proj_w, L1_conv_conv_w, L1_conv_conv_b, L1_conv_x_proj_w, L1_conv_dt_proj_w, L1_conv_dt_proj_b, L1_conv_A_log, L1_conv_D, L1_conv_out_proj_w, L2_conv_weight, L2_conv_bias, L3_conv_weight, L3_conv_bias):
    import jax
    import jax.numpy as jnp

    def _L0_conv_ref(img):
        import jax, jax.numpy as jnp
        import numpy as np
        KERNEL = np.ones((3, 3), dtype=np.float32)
        BORDER_VAL = -2.0
        'Morphological dilation.\n\n            Faithful to the torch module: it pads with border_val=-2, unfolds every\n            k*k window via an identity-kernel conv2d with bias = mask.flip(0), then\n            takes the channel max. That is mathematically:\n                out[y, x] = max_{r, c} padded[y + r, x + c] + bias2d[r, c]\n            where bias2d is the 180-degree-rotated mask (0 where kernel==1,\n            border_val where kernel==0). We compute this directly with k*k shifted\n            slices -- no 9x im2col intermediate, no matmul.\n            '
        kh, kw = KERNEL.shape
        H, W = (img.shape[-2], img.shape[-1])
        padded = jnp.pad(img, ((0, 0), (0, 0), (kh // 2, kh - kh // 2 - 1), (kw // 2, kw - kw // 2 - 1)), mode='constant', constant_values=BORDER_VAL)
        mask = np.where(KERNEL == 0, BORDER_VAL, 0.0).astype(np.float32)
        bias2d = mask[::-1, ::-1]
        out = None
        for r in range(kh):
            for c in range(kw):
                win = padded[..., r:r + H, c:c + W] + bias2d[r, c]
                out = win if out is None else jnp.maximum(out, win)
        return out

    def _L1_conv_ref(x, ln_gamma, ln_beta, in_proj_w, conv_w, conv_b, x_proj_w, dt_proj_w, dt_proj_b, A_log, D, out_proj_w):
        import jax, jax.numpy as jnp
        import numpy as np
        from jax import lax
        R = 4
        C_IN = 8
        D_MODEL = C_IN * R * R
        D_STATE = 32
        D_INNER = 2 * D_MODEL
        D_CONV = 4
        DT_RANK = (D_MODEL + 15) // 16
        B, H, W = (16, 128, 128)

        def _pixel_unshuffle(x, r):
            b, c, h, w = x.shape
            x = x.reshape(b, c, h // r, r, w // r, r)
            x = x.transpose(0, 1, 3, 5, 2, 4)
            return x.reshape(b, c * r * r, h // r, w // r)

        def _pixel_shuffle(x, r):
            b, cr, h, w = x.shape
            c = cr // (r * r)
            x = x.reshape(b, c, r, r, h, w)
            x = x.transpose(0, 1, 4, 2, 5, 3)
            return x.reshape(b, c, h * r, w * r)

        def _layernorm(x, gamma, beta, eps=1e-05):
            mu = jnp.mean(x, axis=-1, keepdims=True)
            var = jnp.mean(jnp.square(x - mu), axis=-1, keepdims=True)
            return (x - mu) * lax.rsqrt(var + eps) * gamma + beta

        def _mamba(u, in_proj_w, conv_w, conv_b, x_proj_w, dt_proj_w, dt_proj_b, A_log, D, out_proj_w):
            xz = jnp.einsum('bld,ed->ble', u, in_proj_w)
            x_in, z = jnp.split(xz, 2, axis=-1)
            xc = x_in.transpose(0, 2, 1)
            xc = jnp.pad(xc, ((0, 0), (0, 0), (D_CONV - 1, 0)))
            xc = lax.conv_general_dilated(xc, conv_w, (1,), 'VALID', dimension_numbers=('NCH', 'OIH', 'NCH'), feature_group_count=D_INNER)
            xc = jax.nn.silu(xc.transpose(0, 2, 1) + conv_b)
            x_dbl = jnp.einsum('bld,ed->ble', xc, x_proj_w)
            dt, Bc, Cc = jnp.split(x_dbl, [DT_RANK, DT_RANK + D_STATE], axis=-1)
            dt = jax.nn.softplus(jnp.einsum('blr,dr->bld', dt, dt_proj_w) + dt_proj_b)
            A = -jnp.exp(A_log)

            def step(h, inputs):
                dt_t, x_t, B_t, C_t = inputs
                h = h * jnp.exp(dt_t[..., None] * A) + (dt_t * x_t)[..., None] * B_t[:, None, :]
                y = jnp.einsum('bds,bs->bd', h, C_t)
                return (h, y)
            h0 = jnp.zeros((u.shape[0], D_INNER, D_STATE), u.dtype)
            _, ys = lax.scan(step, h0, (dt.transpose(1, 0, 2), xc.transpose(1, 0, 2), Bc.transpose(1, 0, 2), Cc.transpose(1, 0, 2)))
            y = ys.transpose(1, 0, 2) + xc * D
            y = y * jax.nn.silu(z)
            return jnp.einsum('bld,ed->ble', y, out_proj_w)
        b, c, h, w = x.shape
        res = x
        u = _pixel_unshuffle(x, R)
        hh, ww = (h // R, w // R)
        u = u.reshape(b, D_MODEL, hh * ww).transpose(0, 2, 1)
        u = _layernorm(u, ln_gamma, ln_beta)
        u = _mamba(u, in_proj_w, conv_w, conv_b, x_proj_w, dt_proj_w, dt_proj_b, A_log, D, out_proj_w)
        u = u.transpose(0, 2, 1).reshape(b, D_MODEL, hh, ww)
        out = _pixel_shuffle(u, R)
        return out + res

    def _L2_conv_ref(input, weight, bias):
        import jax, jax.numpy as jnp
        import numpy as np
        import math
        B, C_IN, C_OUT = (32, 8, 8)
        H, W = (512, 512)
        KH, KW = (3, 3)
        STRIDE = 1
        PAD = 1
        out = jax.lax.conv_general_dilated(input, weight, window_strides=(STRIDE, STRIDE), padding=[(PAD, PAD), (PAD, PAD)], dimension_numbers=('NCHW', 'OIHW', 'NCHW'))
        return out + bias[None, :, None, None]

    def _L3_conv_ref(input, weight, bias):
        import jax, jax.numpy as jnp
        import numpy as np
        import math
        B, C_IN, C_OUT = (32, 8, 8)
        H, W = (512, 512)
        KH, KW = (3, 3)
        STRIDE = 1
        PAD = 1
        out = jax.lax.conv_general_dilated(input, weight, window_strides=(STRIDE, STRIDE), padding=[(PAD, PAD), (PAD, PAD)], dimension_numbers=('NCHW', 'OIHW', 'NCHW'))
        return out + bias[None, :, None, None]

    def _gn(v, G=4, eps=1e-05):
        B_, C_, H_, W_ = v.shape
        g = v.reshape(B_, G, C_ // G, H_, W_)
        m = jnp.mean(g, axis=(2, 3, 4), keepdims=True)
        s = jnp.var(g, axis=(2, 3, 4), keepdims=True)
        return ((g - m) / jnp.sqrt(s + eps)).reshape(v.shape)

    def _ln_c(v, eps=1e-06):
        m = jnp.mean(v, axis=1, keepdims=True)
        s = jnp.var(v, axis=1, keepdims=True)
        return (v - m) / jnp.sqrt(s + eps)

    def _ln_t(v, eps=1e-05):
        m = jnp.mean(v, axis=-1, keepdims=True)
        s = jnp.var(v, axis=-1, keepdims=True)
        return (v - m) / jnp.sqrt(s + eps)

    def _to_tokens(v):
        B_, C_, H_, W_ = v.shape
        return v.reshape(B_, C_, H_ * W_).transpose(0, 2, 1)

    def _from_tokens(t, like):
        B_, C_, H_, W_ = like.shape
        return t.transpose(0, 2, 1).reshape(B_, C_, H_, W_)
    x = x + _L0_conv_ref(_gn(x))
    x = x + _L1_conv_ref(_gn(x), L1_conv_ln_gamma, L1_conv_ln_beta, L1_conv_in_proj_w, L1_conv_conv_w, L1_conv_conv_b, L1_conv_x_proj_w, L1_conv_dt_proj_w, L1_conv_dt_proj_b, L1_conv_A_log, L1_conv_D, L1_conv_out_proj_w)
    x = x + _L2_conv_ref(_gn(x), L2_conv_weight, L2_conv_bias)
    x = x + _L3_conv_ref(_gn(x), L3_conv_weight, L3_conv_bias)
    return x

_drawn_inputs = setup_inputs


def setup_inputs(seed=0):
    import zlib

    import numpy as np

    out = dict(_drawn_inputs(seed))
    spreads = {'L1_conv_ln_gamma': (1.0, 0.2), 'L1_conv_ln_beta': (0.0, 0.1), 'L1_conv_D': (1.0, 0.2)}
    factors = {'L1_conv_conv_b': 4.794, 'L3_conv_bias': 2.715}
    for name, (base, spread) in spreads.items():
        noise = np.random.default_rng([zlib.crc32(name.encode()), seed]).standard_normal(out[name].shape)
        drawn = base * np.exp(spread * noise) if base else spread * noise
        out[name] = jnp.asarray(drawn.astype(out[name].dtype))
    for name, factor in factors.items():
        out[name] = (out[name] * factor).astype(out[name].dtype)
    return out
```

```python
from contextlib import ExitStack

import concourse.bass as bass
from concourse import mybir

F32 = mybir.dt.float32
BF16 = mybir.dt.bfloat16
ALU = mybir.AluOpType
ACT = mybir.ActivationFunctionType

P = 128
B, C, H, W = 16, 8, 256, 256
R = 4
TH, TW = H // R, W // R
L = TH * TW
BAND = H // (P // C)
T = 512
NC = L // T
TROWS = T // TW
DI = 256
NH = DI // P
S = 32
DTR = 8
TAPS = 4
PAD = TAPS - 1
XR = 2 * S + DTR
BORDER = -2.0
EPS = 1e-5
RING = 2
LAG = 3


def scratch_order():
    order = [("gn_mean", 0), ("gn_var", 0), ("gn_mean", 1), ("gn_var", 1)]
    order += prologue_uses(0)
    for c in range(NC):
        for s in range(S):
            order += scratch_at(c, s)
    order += [("out", NC - 1), ("gn_mean", 2), ("gn_var", 2)] + [("conv0", k) for k in range(NC)]
    order += [("gn_mean", 3), ("gn_var", 3)] + [("conv1", k) for k in range(NC)]
    return order


def prologue_uses(c):
    return [("center", c), ("var", c), ("x", c, 0), ("x", c, 1), ("z", c, 0), ("z", c, 1),
            ("xproj", c), ("dt", c, 0), ("dt", c, 1)]


SLOT = {0: ("center",), 2: ("var",), 6: ("x", 0), 8: ("x", 1), 10: ("z", 0), 12: ("z", 1),
        16: ("xproj",), 19: ("dt", 0), 21: ("dt", 1)}
OUT_SLOT = 4


def scratch_at(c, s):
    uses = []
    if s in SLOT and c + 1 < NC:
        name, *half = SLOT[s]
        uses.append((name, c + 1, *half))
    if s == OUT_SLOT and c > 0:
        uses.append(("out", c - 1))
    return uses


ORDER = scratch_order()
USES = len(ORDER)


def build(nc, x, scan_w, conv_w3, conv_b3, const, out):
    patch_scratch = nc.dram_tensor("patch_scratch", (C, H // R, R, R, TW), F32, kind="Internal").ap()
    rows_scratch = nc.dram_tensor("rows_scratch", (C, H // R, R, R, TW), F32, kind="Internal").ap()
    with ExitStack() as ctx:
        def sb(name, shape, dt=F32):
            return ctx.enter_context(nc.sbuf_tensor(name, shape, dt))

        def ps(name, shape):
            return ctx.enter_context(nc.psum_tensor(name, shape, F32))

        def sem(name):
            return ctx.enter_context(nc.semaphore(name))

        center_m = sb("center_m", [P, P])
        mean_m = sb("mean_m", [P, P])
        ident = sb("ident", [P, P])
        group_m = sb("group_m", [P, P])
        halo_keep = sb("halo_keep", [P, 4])
        select = sb("select", [3 * S, S * P], BF16)
        w_x = sb("w_x", [P, TAPS, DI])
        w_z = sb("w_z", [P, DI])
        w_xp = sb("w_xp", [P, NH, XR])
        w_dt = sb("w_dt", [2 * S + DTR, DI])
        w_out = sb("w_out", [P, NH, P])
        conv_bias = sb("conv_bias", [P, NH])
        dt_bias = sb("dt_bias", [P, NH])
        d_skip = sb("d_skip", [P, NH])
        a_neg = sb("a_neg", [P, NH * S])
        gamma = sb("gamma", [P, 1])
        beta = sb("beta", [P, 1])
        w_conv = [sb(f"w_conv{n}", [P, 9, P]) for n in range(2)]
        b_conv = [sb(f"b_conv{n}", [P, 1]) for n in range(2)]
        eps_col = sb("eps_col", [P, 1])

        raw = sb("raw", [P, BAND + 2, W])
        norm = sb("norm", [P, R + 2, W + 2])
        vmax = sb("vmax", [P, R, W + 2])
        x1 = sb("x1", [P, L])
        g1 = sb("g1", [P, L])
        x2 = sb("x2", [P, L])
        padded = sb("padded", [P, TH + 2, TW + 2])
        stats = sb("stats", [P, NC, 6])
        mv = sb("mv", [P, 2])
        gsmall = sb("gsmall", [P, 10])

        u_ln = sb("u_ln", [P, PAD + T])
        cen = sb("cen", [P, T])
        sq = sb("sq", [P, T])
        rstd = sb("rstd", [P, T])
        xz = sb("xz", [P, 2, NH, T])
        xc = sb("xc", [P, 2, NH, T])
        zs = sb("zs", [P, 2, NH, T])
        dt = sb("dt", [P, 2, NH, T])
        dtx = sb("dtx", [P, 2, NH, T])
        rest = sq[0:2 * S, :]
        parts = sb("parts", [2 * S, 3, T], BF16)
        dt_rows = cen
        b_parts = sb("b_parts", [3 * S, 2, T], BF16)
        c_parts = sb("c_parts", [3 * S, 2, T], BF16)
        u_in = sb("u_in", [P, RING, NH, T])
        h = sb("h", [P, RING, NH, T])
        hc = sb("hc", [P, RING, NH, T])
        c_sb = sb("c_sb", [P, RING, T])
        carry = sb("carry", [P, NH, S])

        scratch = ps("scratch", [P, T])
        b_ps = ps("b_ps", [P, 2, T])
        c_ps = ps("c_ps", [P, T])
        a_ps = ps("a_ps", [P, NH, T])
        y_ps = ps("y_ps", [P, NH, T])

        weights_in = sem("weights_in")
        select_in = sem("select_in")
        setup_v = sem("setup_v")
        setup_a = sem("setup_a")
        setup_p = sem("setup_p")
        filled = sem("scratch_filled")
        emptied = sem("scratch_emptied")
        raw_in = sem("raw_in")
        dil = sem("dilation_steps")
        x1_rows_out = sem("x1_rows_out")
        x1_in = sem("x1_patch_in")
        st = sem("group_stats")
        gs = sem("group_small_v")
        ga = sem("group_small_a")
        g1_done = sem("g1_done")
        x1_sum = sem("x1_plus_g1")
        padded_done = sem("padded_done")
        x4_out = sem("x4_patch_out")
        x4_in = sem("x4_rows_in")
        x4_woven = sem("x4_interleaved")
        stored = sem("stored")
        carry_u = sem("u_tail_kept")
        rstd_done = sem("rstd_done")
        scaled = sem("token_scaled")
        u_done = sem("u_ln_done")
        silu_done = sem("silu_done")
        hi_done = sem("part_hi")
        mid_done = sem("part_mid")
        lo_done = sem("part_lo")
        parts_in = sem("parts_moved")
        exp_done = sem("dt_exp")
        ln_done = sem("dt_ln")
        dt_done = sem("dt_done")
        dtx_done = sem("dtx_done")
        b_cast = sem("b_broadcast")
        c_cast = sem("c_broadcast")
        u_made = sem("state_input")
        a_made = sem("decay")
        c_copied = sem("c_copied")
        h_done = sem("h_done")
        kept = sem("carry_kept")
        hc_done = sem("hc_done")
        summed = sem("y_summed")
        skip_done = sem("y_plus_skip")
        gated = sem("y_gated")

        block = ctx.enter_context(nc.Block())

        def used(b, *use):
            return b * USES + ORDER.index(use) + 1

        def read(b, *use):
            return used(b, *use) + 1

        def chunk(b, c, n=1):
            return (b * NC + c + 1) * n

        def state(b, c, s, n=1):
            return ((b * NC + c) * S + s + 1) * n

        def behind(c, s, n):
            at = c * S + s - n
            return at // S, at % S

        N_WEIGHTS = 28
        SETUP_V = 3 + TAPS + 2 * (9 + 8)
        SETUP_P = 3
        BANDS = BAND // R
        DIL_AT = [4 + 6 * (k + 1) + 1 + (k == BANDS - 1) for k in range(BANDS)]
        DIL = DIL_AT[-1]
        GS = 5

        @block.sync
        def _(sp):
            def load(dst, src):
                sp.dma_start(dst, src).then_inc(weights_in, 16)

            load(center_m[:, :], const["center"])
            load(mean_m[:, :], const["mean"])
            load(ident[:, :], const["ident"])
            load(group_m[:, :], const["group"])
            load(halo_keep[:, :], const["halo"])
            load(w_x[:, 0, :], scan_w["in_x_t"])
            load(w_z[:, :], scan_w["in_z_t"])
            for half in range(NH):
                rows = slice(half * P, (half + 1) * P)
                load(w_xp[:, half, :], scan_w["x_proj_t"][rows, :])
                load(w_out[:, half, :], scan_w["out_proj_t"][rows, :])
                load(conv_bias[:, half:half + 1], scan_w["conv_b"][rows, :])
                load(dt_bias[:, half:half + 1], scan_w["dt_b"][rows, :])
                load(d_skip[:, half:half + 1], scan_w["d"][rows, :])
                load(a_neg[:, half * S:(half + 1) * S], scan_w["a_log"][rows, :])
            load(w_dt[2 * S:, :], scan_w["dt_proj_t"])
            load(gamma[:, :], scan_w["gamma"])
            load(beta[:, :], scan_w["beta"])
            load(norm[:, 0:TAPS, 0:DI], scan_w["conv_w_t"].partition_broadcast(P))
            for n in range(2):
                load(b_conv[n][:, :], conv_b3[n])
            load(g1[:, 0:72], conv_w3[0])
            load(g1[:, 72:144], conv_w3[1])
            load(x2[:, 0:81 * 16], const["taps"])

            sp.dma_start(x1[0:3 * S, :], const["select"]).then_inc(select_in, 16)

            sp.wait_ge(setup_v, SETUP_V)
            sp.wait_ge(setup_p, SETUP_P)
            sp.wait_ge(setup_a, 2)
            sp.sem_inc(stored, 16)
            with sp.Fori(0, B) as b:
                img = x[bass.ds(b, 1)].rearrange("o c (g r) w -> (o c g) (r w)", r=BAND)
                sp.wait_ge(stored, (b + 1) * 16)
                sp.dma_start(raw[:, 1:BAND + 1, :], img).then_inc(raw_in, 16)
                sp.dma_start(raw[1:P, 0:1, :], img[0:P - 1, (BAND - 1) * W:]).then_inc(raw_in, 16)
                sp.dma_start(raw[0:P - 1, BAND + 1:, :], img[1:P, 0:W]).then_inc(raw_in, 16)
                for k in range(BANDS):
                    sp.wait_ge(dil, b * DIL + DIL_AT[k])
                    sp.dma_start(patch_scratch.rearrange("c (g l) r q w -> l (c g) r (q w)", l=BANDS)[k],
                                 vmax[:, :, 0:W]).then_inc(x1_rows_out, 16)
                sp.wait_ge(x1_rows_out, (b + 1) * BANDS * 16)
                for ch in range(C):
                    sp.dma_start(x1[ch * 16:(ch + 1) * 16, :].rearrange("p (t w) -> p t w", w=TW),
                                 patch_scratch[ch].rearrange("t r q w -> (r q) t w")).then_inc(x1_in, 16)
                for c in range(NC):
                    sp.wait_ge(lo_done, chunk(b, c))
                    for k in range(3):
                        sp.dma_start(b_parts[k * S:(k + 1) * S, c % 2, :], parts[0:S, k, :]).then_inc(parts_in, 16)
                        sp.dma_start(c_parts[k * S:(k + 1) * S, c % 2, :], parts[S:2 * S, k, :]).then_inc(parts_in, 16)
                sp.wait_ge(emptied, read(b, "conv1", NC - 1))
                for ch in range(C):
                    sp.dma_start(rows_scratch[ch].rearrange("t r q w -> (r q) t w"),
                                 x2[ch * 16:(ch + 1) * 16, :].rearrange("p (t w) -> p t w", w=TW)).then_inc(x4_out, 16)
                sp.wait_ge(x4_out, (b + 1) * 16 * C)
                sp.dma_start(g1[:, :], rows_scratch.rearrange("c (g l) r q w -> (c g) (l r q w)", l=BANDS)).then_inc(x4_in, 16)
                sp.wait_ge(x4_woven, b + 1)
                sp.dma_start(out[bass.ds(b, 1)].rearrange("o c (g r) w -> (o c g) (r w)", r=BAND),
                             raw[:, 1:BAND + 1, :]).then_inc(stored, 16)
            sp.wait_ge(stored, (B + 1) * 16)


        @block.gpsimd
        def _(pool):
            pool.memset(raw[:, :, :], 0.0).then_inc(setup_p, 1)
            pool.memset(padded[:, :, :], 0.0).then_inc(setup_p, 1)
            pool.memset(u_ln[:, :], 0.0).then_inc(setup_p, 1)
            with pool.Fori(0, B) as b:
                pool.wait_ge(g1_done, b + 1)
                pool.tensor_tensor(x1[:, :], x1[:, :], g1[:, :], ALU.add).then_inc(x1_sum, 1)

                def scale_tokens(c):
                    pool.wait_ge(rstd_done, chunk(b, c))
                    pool.tensor_tensor(cen[:, :], cen[:, :], rstd[:, :], ALU.mult).then_inc(scaled, 1)

                scale_tokens(0)
                for c in range(NC):
                    for s in range(S):
                        r = s % RING
                        pool.wait_ge(c_copied, state(b, c, s))
                        pool.wait_ge(h_done, state(b, c, s, NH))
                        if c or s >= RING:
                            pool.wait_ge(summed, state(b, *behind(c, s, RING)))
                        pool.tensor_tensor(hc[:, r], h[:, r], c_sb[:, r:r + 1, :].broadcast_to([P, NH, T]),
                                           ALU.mult).then_inc(hc_done, 1)
                        if s == 3 and c + 1 < NC:
                            scale_tokens(c + 1)

        @block.scalar
        def _(act):
            act.wait_ge(weights_in, N_WEIGHTS * 16)
            act.activation(a_neg[:, :], a_neg[:, :], ACT.Exp).then_inc(setup_a, 1)
            act.wait_ge(select_in, 16)
            act.activation(select[:, :], x1[0:3 * S, :], ACT.Copy).then_inc(setup_a, 1)
            with act.Fori(0, B) as b:
                def norm_scale(n):
                    act.wait_ge(filled, used(b, "gn_var", n))
                    act.activation(gsmall[:, 3:4], scratch[:, 0:1], ACT.Ln, bias=eps_col[:, :]).then_inc(emptied, 1)
                    act.wait_ge(emptied, read(b, "gn_var", n))
                    act.activation(gsmall[:, 4:5], gsmall[:, 3:4], ACT.Exp, scale=-0.5).then_inc(ga, 1)

                def centered(c):
                    act.wait_ge(filled, used(b, "center", c))
                    act.activation(cen[:, :], scratch[:, :], ACT.Copy)
                    act.activation(sq[:, :], scratch[:, :], ACT.Square).then_inc(emptied, 1)

                def token_rstd(c):
                    act.wait_ge(filled, used(b, "var", c))
                    act.activation(rstd[:, :], scratch[:, :], ACT.Ln, bias=eps_col[:, :]).then_inc(emptied, 1)
                    act.wait_ge(emptied, read(b, "var", c))
                    act.activation(rstd[:, :], rstd[:, :], ACT.Exp, scale=-0.5).then_inc(rstd_done, 1)

                def layer_norm(c):
                    if c:
                        act.activation(u_ln[:, 0:PAD], u_ln[:, T:T + PAD], ACT.Copy).then_inc(carry_u, 1)
                    else:
                        act.memzero(u_ln[:, 0:PAD]).then_inc(carry_u, 1)
                    act.wait_ge(carry_u, chunk(b, c))
                    act.wait_ge(scaled, chunk(b, c))
                    act.activation(u_ln[:, PAD:], cen[:, :], ACT.Identity, bias=beta[:, :],
                                   scale=gamma[:, :]).then_inc(u_done, 1)

                def silus(c):
                    act.wait_ge(emptied, read(b, "z", c, NH - 1))
                    act.activation(xc[:, c % 2], xz[:, 0], ACT.Silu)
                    act.activation(zs[:, c % 2], xz[:, 1], ACT.Silu).then_inc(silu_done, 1)

                def split_hi(c):
                    act.wait_ge(filled, used(b, "xproj", c))
                    act.activation(dt_rows[2 * S:XR, :], scratch[2 * S:XR, :], ACT.Copy)
                    act.activation(parts[:, 0, :], scratch[0:2 * S, :], ACT.Copy).then_inc(hi_done, 1)

                def split_mid(c):
                    act.wait_ge(emptied, read(b, "xproj", c))
                    act.activation(parts[:, 1, :], rest[:, :], ACT.Copy).then_inc(mid_done, 1)

                def softplus_in(c, half):
                    act.wait_ge(filled, used(b, "dt", c, half))
                    act.activation(xz[:, 0, half], scratch[:, :], ACT.Abs, bias=dt_bias[:, half:half + 1])
                    act.activation(xz[:, 1, half], scratch[:, :], ACT.Relu,
                                   bias=dt_bias[:, half:half + 1]).then_inc(emptied, 1)

                def softplus_log(c):
                    act.wait_ge(emptied, read(b, "dt", c, NH - 1))
                    act.activation(xz[:, 0], xz[:, 0], ACT.Exp, scale=-1.0).then_inc(exp_done, 1)
                    act.wait_ge(exp_done, chunk(b, c))
                    act.activation(xz[:, 0], xz[:, 0], ACT.Ln, bias=1.0).then_inc(ln_done, 1)

                def keep(c, s):
                    act.wait_ge(h_done, state(b, c, s, NH))
                    act.activation(carry[:, :, s:s + 1], h[:, s % RING, :, T - 1:T], ACT.Copy).then_inc(kept, 1)

                norm_scale(0)
                norm_scale(1)
                centered(0)
                token_rstd(0)
                layer_norm(0)
                silus(0)
                split_hi(0)
                split_mid(0)
                softplus_in(0, 0)
                softplus_in(0, 1)
                softplus_log(0)
                for c in range(NC):
                    act.wait_ge(dt_done, chunk(b, c))
                    for s in range(S):
                        r = s % RING
                        for half in range(NH):
                            if c or s:
                                act.wait_ge(h_done, state(b, *behind(c, s, 1), NH) - (NH - 1 - half))
                            at = half * S + s
                            act.activation(a_ps[:, half], dt[:, c % 2, half], ACT.Exp,
                                           scale=a_neg[:, at:at + 1]).then_inc(a_made, 1)
                        act.wait_ge(c_cast, state(b, c, s))
                        if c or s >= RING:
                            act.wait_ge(hc_done, state(b, *behind(c, s, RING)))
                        act.activation(c_sb[:, r], c_ps[:, :], ACT.Copy).then_inc(c_copied, 1)
                        if c or s:
                            keep(*behind(c, s, 1))
                        if c + 1 < NC:
                            if s == 1:
                                centered(c + 1)
                            if s == 3:
                                token_rstd(c + 1)
                            if s == 4:
                                layer_norm(c + 1)
                            if s == 14:
                                silus(c + 1)
                            if s == 17:
                                split_hi(c + 1)
                            if s == 19:
                                split_mid(c + 1)
                            if s == 20:
                                softplus_in(c + 1, 0)
                            if s == 22:
                                softplus_in(c + 1, 1)
                                softplus_log(c + 1)
                keep(NC - 1, S - 1)
                norm_scale(2)
                norm_scale(3)
                act.wait_ge(x4_in, (b + 1) * 16)
                act.activation(raw[:, 1:BAND + 1, :].rearrange("p r (w q) -> p r q w", q=R),
                               g1[:, :].rearrange("p (r q w) -> p r q w", q=R, r=BAND),
                               ACT.Copy).then_inc(x4_woven, 1)

        @block.tensor
        def _(pe):
            pe.wait_ge(weights_in, N_WEIGHTS * 16)
            pe.wait_ge(setup_v, SETUP_V)
            pe.wait_ge(setup_a, 2)
            with pe.Fori(0, B) as b:
                def take_scratch(*use):
                    pe.wait_ge(emptied, used(b, *use))

                def group_mean(n):
                    pe.wait_ge(gs, (b * 4 + n) * GS + 1)
                    take_scratch("gn_mean", n)
                    pe.matmul(scratch[:, 0:1], group_m[:, :], mv[:, 0:1], start=True, stop=True).then_inc(filled, 1)
                    pe.wait_ge(gs, (b * 4 + n) * GS + 4)
                    take_scratch("gn_var", n)
                    pe.matmul(scratch[:, 0:1], group_m[:, :], gsmall[:, 2:3], start=True, stop=True).then_inc(filled, 1)

                def center(c):
                    if c == 0:
                        pe.wait_ge(g1_done, b + 1)
                    take_scratch("center", c)
                    pe.matmul(scratch[:, :], center_m[:, :], g1[:, c * T:(c + 1) * T],
                              start=True, stop=True).then_inc(filled, 1)

                def variance(c):
                    take_scratch("var", c)
                    pe.matmul(scratch[:, :], mean_m[:, :], sq[:, :], start=True, stop=True).then_inc(filled, 1)

                def project_x(c, half):
                    pe.wait_ge(u_done, chunk(b, c))
                    take_scratch("x", c, half)
                    for k in range(TAPS):
                        mm = pe.matmul(scratch[:, :], w_x[:, k, half * P:(half + 1) * P], u_ln[:, k:k + T],
                                       start=(k == 0), stop=(k == TAPS - 1))
                    mm.then_inc(filled, 1)

                def project_z(c, half):
                    take_scratch("z", c, half)
                    pe.matmul(scratch[:, :], w_z[:, half * P:(half + 1) * P], u_ln[:, PAD:],
                              start=True, stop=True).then_inc(filled, 1)

                def x_proj(c):
                    pe.wait_ge(silu_done, chunk(b, c))
                    take_scratch("xproj", c)
                    for half in range(NH):
                        mm = pe.matmul(scratch[0:XR, :], w_xp[:, half, :], xc[:, c % 2, half],
                                       start=(half == 0), stop=(half == NH - 1))
                    mm.then_inc(filled, 1)

                def dt_proj(c, half):
                    pe.wait_ge(hi_done, chunk(b, c))
                    take_scratch("dt", c, half)
                    pe.matmul(scratch[:, :], w_dt[2 * S:, half * P:(half + 1) * P], dt_rows[2 * S:XR, :],
                              start=True, stop=True).then_inc(filled, 1)

                def out_proj(c):
                    pe.wait_ge(gated, chunk(b, c))
                    take_scratch("out", c)
                    for half in range(NH):
                        mm = pe.matmul(scratch[:, :], w_out[:, half, :], xc[:, c % 2, half],
                                       start=(half == 0), stop=(half == NH - 1))
                    mm.then_inc(filled, 1)

                def sum_states(c, s):
                    pe.wait_ge(hc_done, state(b, c, s))
                    if s == 0 and c:
                        pe.wait_ge(skip_done, chunk(b, c - 1, NH))
                    for half in range(NH):
                        mm = pe.matmul(y_ps[:, half], ident[:, :], hc[:, s % RING, half],
                                       start=(s == 0), stop=(s == S - 1), skip_group_check=True)
                    mm.then_inc(summed, 1)

                def scratch_use(use):
                    name, c, *half = use
                    {"center": center, "var": variance, "x": project_x, "z": project_z, "xproj": x_proj,
                     "dt": dt_proj, "out": out_proj}[name](c, *half)

                def convolve(n, k):
                    take_scratch(f"conv{n}", k)
                    for tap in range(9):
                        dh, dw = tap // 3, tap % 3
                        mm = pe.matmul(scratch[:, :].rearrange("p (a w) -> p a w", w=TW), w_conv[n][:, tap, :],
                                       padded[:, k * TROWS + dh:(k + 1) * TROWS + dh, dw:dw + TW],
                                       start=(tap == 0), stop=(tap == 8))
                    mm.then_inc(filled, 1)

                group_mean(0)
                group_mean(1)
                for use in prologue_uses(0):
                    scratch_use(use)
                for c in range(NC):
                    pe.wait_ge(parts_in, chunk(b, c, 6 * 16))
                    for s in range(S):
                        sel = select[:, s * P:(s + 1) * P]
                        if c or s >= 2:
                            pe.wait_ge(u_made, state(b, *behind(c, s, 2)))
                        pe.matmul(b_ps[:, s % 2], sel, b_parts[:, c % 2, :], start=True, stop=True).then_inc(b_cast, 1)
                        if c or s:
                            pe.wait_ge(c_copied, state(b, *behind(c, s, 1)))
                        pe.matmul(c_ps[:, :], sel, c_parts[:, c % 2, :], start=True, stop=True).then_inc(c_cast, 1)
                        if c or s >= LAG:
                            sum_states(*behind(c, s, LAG))
                        for use in scratch_at(c, s):
                            scratch_use(use)
                for s in range(S - LAG, S):
                    sum_states(NC - 1, s)
                out_proj(NC - 1)
                for n in range(2):
                    group_mean(2 + n)
                    pe.wait_ge(padded_done, b * 2 + n + 1)
                    for k in range(NC):
                        convolve(n, k)

        @block.vector
        def _(dve):
            steps = 0

            def own(ins):
                nonlocal steps
                steps += 1
                ins.then_inc(setup_v, 1)
                dve.wait_ge(setup_v, steps)

            own(dve.memset(eps_col[:, :], EPS))
            dve.wait_ge(weights_in, N_WEIGHTS * 16)
            dve.wait_ge(setup_a, 1)
            own(dve.tensor_scalar(a_neg[:, :], a_neg[:, :], -1.0, None, ALU.mult))
            for k in reversed(range(TAPS)):
                own(dve.tensor_tensor(w_x[:, k, :], w_x[:, 0, :], norm[:, k, 0:DI], ALU.mult))
            own(dve.memset(norm[:, :, :], BORDER))
            product = xz[:, :, :, :].rearrange("p a h t -> p (a h t)")[:, 0:9 * P]
            for n in range(2):
                for j in range(9):
                    w = g1[:, 72 * n + 8 * j:72 * n + 8 * (j + 1)].unsqueeze(1).unsqueeze(3)
                    at = x2[:, 144 * j:144 * (j + 1)].rearrange("p (t m) -> p t m", t=9).unsqueeze(2)
                    dst = (w_conv[n][:, :, :] if j == 0 else product.rearrange("p (t k) -> p t k", t=9))
                    own(dve.tensor_tensor(dst.rearrange("p t (c m) -> p t c m", c=C),
                                          w.broadcast_to([P, 9, C, 16]), at.broadcast_to([P, 9, C, 16]), ALU.mult))
                    if j:
                        flat = w_conv[n][:, :, :].rearrange("p t k -> p (t k)")
                        own(dve.tensor_tensor(flat, flat, product, ALU.add))
            dve.sem_inc(emptied, 1)
            with dve.Fori(0, B) as b:
                dil_at = 0

                def dilate(ins):
                    nonlocal dil_at
                    dil_at += 1
                    ins.then_inc(dil, 1)
                    dve.wait_ge(dil, b * DIL + dil_at)

                def group_norm(n, src):
                    for k in range(NC):
                        last = dve.bn_stats(stats[:, k, :], src(k))
                    last.then_inc(st, 1)
                    at = (b * 4 + n) * GS
                    dve.wait_ge(st, b * 4 + n + 1)
                    dve.memset(gsmall[:, 2:3], 0.0)
                    dve.bn_aggr(mv[:, :], stats[:, :, :]).then_inc(gs, 1)
                    dve.wait_ge(filled, used(b, "gn_mean", n))
                    dve.tensor_copy(gsmall[:, 0:1], scratch[:, 0:1]).then_inc(gs, 1)
                    dve.wait_ge(gs, at + 2)
                    dve.tensor_tensor(gsmall[:, 1:2], mv[:, 0:1], gsmall[:, 0:1], ALU.subtract).then_inc(gs, 1)
                    dve.wait_ge(gs, at + 3)
                    dve.scalar_tensor_tensor(out=gsmall[:, 2:3], in0=gsmall[:, 1:2], scalar=gsmall[:, 1:2],
                                             in1=mv[:, 1:2], op0=ALU.mult, op1=ALU.add).then_inc(gs, 1)
                    dve.wait_ge(gs, at + 4)
                    dve.sem_inc(emptied, 1)
                    dve.wait_ge(ga, b * 4 + n + 1)
                    dve.tensor_scalar(gsmall[:, 5:6], gsmall[:, 0:1], gsmall[:, 4:5], -1.0,
                                      ALU.mult, ALU.mult).then_inc(gs, 1)
                    dve.wait_ge(gs, at + 5)

                def normed(dst, src):
                    return dve.tensor_scalar(dst, src, gsmall[:, 4:5], gsmall[:, 5:6], ALU.mult, ALU.add)

                def make_u(c, s):
                    if s == 0:
                        dve.wait_ge(dtx_done, chunk(b, c))
                    dve.wait_ge(b_cast, state(b, c, s))
                    if c or s >= RING:
                        dve.wait_ge(h_done, state(b, *behind(c, s, RING), NH))
                    dve.tensor_tensor(u_in[:, s % RING], dtx[:, c % 2],
                                      b_ps[:, s % 2:s % 2 + 1, :].broadcast_to([P, NH, T]), ALU.mult).then_inc(u_made, 1)

                def scan(c, s):
                    r = s % RING
                    if c or s >= RING:
                        dve.wait_ge(hc_done, state(b, *behind(c, s, RING)))
                        dve.wait_ge(kept, state(b, *behind(c, s, RING)))
                    dve.wait_ge(u_made, state(b, c, s))
                    for half in range(NH):
                        dve.wait_ge(a_made, state(b, c, s, NH) - (NH - 1 - half))
                        start = carry[:, half, s:s + 1] if c else 0.0
                        dve.tensor_tensor_scan(h[:, r, half], a_ps[:, half], u_in[:, r, half], start,
                                               ALU.mult, ALU.add).then_inc(h_done, 1)

                def copy_x(c, half):
                    dve.wait_ge(filled, used(b, "x", c, half))
                    dve.tensor_scalar(xz[:, 0, half], scratch[:, :], conv_bias[:, half:half + 1], None,
                                      ALU.add).then_inc(emptied, 1)

                def copy_z(c, half):
                    dve.wait_ge(filled, used(b, "z", c, half))
                    dve.tensor_copy(xz[:, 1, half], scratch[:, :]).then_inc(emptied, 1)

                def split_rest(c):
                    dve.wait_ge(hi_done, chunk(b, c))
                    dve.tensor_tensor(rest[:, :], scratch[0:2 * S, :], parts[:, 0, :], ALU.subtract).then_inc(emptied, 1)

                def split_lo(c):
                    dve.wait_ge(mid_done, chunk(b, c))
                    dve.tensor_tensor(parts[:, 2, :], rest[:, :], parts[:, 1, :], ALU.subtract).then_inc(lo_done, 1)

                def softplus_sum(c):
                    dve.wait_ge(ln_done, chunk(b, c))
                    dve.tensor_tensor(dt[:, c % 2], xz[:, 0], xz[:, 1], ALU.add).then_inc(dt_done, 1)

                def dt_times_x(c):
                    dve.wait_ge(dt_done, chunk(b, c))
                    dve.wait_ge(silu_done, chunk(b, c))
                    dve.tensor_tensor(dtx[:, c % 2], dt[:, c % 2], xc[:, c % 2], ALU.mult).then_inc(dtx_done, 1)

                def gate(c):
                    dve.wait_ge(summed, state(b, c, S - 1))
                    for half in range(NH):
                        dve.scalar_tensor_tensor(out=xc[:, c % 2, half], in0=xc[:, c % 2, half],
                                                 scalar=d_skip[:, half:half + 1], in1=y_ps[:, half],
                                                 op0=ALU.mult, op1=ALU.add).then_inc(skip_done, 1)
                    dve.wait_ge(skip_done, chunk(b, c, NH))
                    dve.tensor_tensor(xc[:, c % 2], xc[:, c % 2], zs[:, c % 2], ALU.mult).then_inc(gated, 1)

                def residual(c):
                    dve.wait_ge(filled, used(b, "out", c))
                    dve.wait_ge(x1_sum, b + 1)
                    part = slice(c * T, (c + 1) * T)
                    dve.tensor_tensor(x2[:, part], x1[:, part], scratch[:, :], ALU.add).then_inc(emptied, 1)

                dve.wait_ge(raw_in, (b + 1) * 3 * 16)
                group_norm(0, lambda k: raw[:, 1 + 2 * k:3 + 2 * k, :].rearrange("p a w -> p (a w)"))
                for side in range(2):
                    keep, fill = halo_keep[:, 2 * side:2 * side + 1], halo_keep[:, 2 * side + 1:2 * side + 2]
                    dilate(dve.tensor_scalar(gsmall[:, 6 + 2 * side:7 + 2 * side], keep, gsmall[:, 4:5], None, ALU.mult))
                    dilate(dve.scalar_tensor_tensor(out=gsmall[:, 7 + 2 * side:8 + 2 * side], in0=keep,
                                                    scalar=gsmall[:, 5:6], in1=fill, op0=ALU.mult, op1=ALU.add))
                inner = slice(1, W + 1)
                for k in range(BANDS):
                    first, last = (1 if k == 0 else 0), (R + 1 if k == BANDS - 1 else R + 2)
                    if k:
                        dve.wait_ge(x1_rows_out, (b * BANDS + k) * 16)
                    dilate(normed(norm[:, first:last, inner], raw[:, k * R + first:k * R + last, :]))
                    if k in (0, BANDS - 1):
                        side, row = (0, 0) if k == 0 else (1, R + 1)
                        dilate(dve.tensor_scalar(norm[:, row:row + 1, inner], raw[:, k * R + row:k * R + row + 1, :],
                                                 gsmall[:, 6 + 2 * side:7 + 2 * side],
                                                 gsmall[:, 7 + 2 * side:8 + 2 * side], ALU.mult, ALU.add))
                    dilate(dve.tensor_tensor(vmax[:, :, :], norm[:, 0:R, :], norm[:, 1:R + 1, :], ALU.max))
                    dilate(dve.tensor_tensor(vmax[:, :, :], vmax[:, :, :], norm[:, 2:R + 2, :], ALU.max))
                    top = norm[:, 1:R + 1, inner]
                    dilate(dve.tensor_tensor(top, vmax[:, :, 0:W], vmax[:, :, 1:W + 1], ALU.max))
                    dilate(dve.tensor_tensor(top, top, vmax[:, :, 2:W + 2], ALU.max))
                    dilate(dve.tensor_tensor(vmax[:, :, 0:W].rearrange("p r (q w) -> p r q w", q=R),
                                             top.rearrange("p r (w q) -> p r q w", q=R),
                                             raw[:, k * R + 1:(k + 1) * R + 1, :].rearrange("p r (w q) -> p r q w", q=R),
                                             ALU.add))
                dve.wait_ge(x1_in, (b + 1) * C * 16)
                group_norm(1, lambda k: x1[:, k * T:(k + 1) * T])
                normed(g1[:, :], x1[:, :]).then_inc(g1_done, 1)
                copy_x(0, 0)
                copy_x(0, 1)
                copy_z(0, 0)
                copy_z(0, 1)
                split_rest(0)
                split_lo(0)
                softplus_sum(0)
                dt_times_x(0)
                make_u(0, 0)
                for c in range(NC):
                    for s in range(S):
                        if s + 1 < S or c + 1 < NC:
                            make_u(*behind(c, s, -1))
                        scan(c, s)
                        if c > 0:
                            if s == 1:
                                gate(c - 1)
                            if s == 5:
                                residual(c - 1)
                        if c + 1 < NC:
                            if s in (7, 9):
                                copy_x(c + 1, (s - 7) // 2)
                            if s in (11, 13):
                                copy_z(c + 1, (s - 11) // 2)
                            if s == 18:
                                split_rest(c + 1)
                            if s == 20:
                                split_lo(c + 1)
                            if s == 24:
                                softplus_sum(c + 1)
                            if s == 25:
                                dt_times_x(c + 1)
                gate(NC - 1)
                residual(NC - 1)
                dve.wait_ge(emptied, read(b, "out", NC - 1))
                for n in range(2):
                    group_norm(2 + n, lambda k: x2[:, k * T:(k + 1) * T])
                    normed(padded[:, 1:TH + 1, 1:TW + 1],
                           x2[:, :].rearrange("p (t w) -> p t w", w=TW)).then_inc(padded_done, 1)
                    for k in range(NC):
                        part = slice(k * T, (k + 1) * T)
                        dve.wait_ge(filled, used(b, f"conv{n}", k))
                        dve.scalar_tensor_tensor(out=x2[:, part], in0=scratch[:, :], scalar=b_conv[n][:, :],
                                                 in1=x2[:, part], op0=ALU.add, op1=ALU.add).then_inc(emptied, 1)
                    dve.wait_ge(emptied, read(b, f"conv{n}", NC - 1))


def tables():
    import numpy as np

    group = np.kron(np.eye(4), np.full((32, 32), 1 / 32))
    select = np.tile(np.kron(np.eye(S), np.ones((1, P))), (3, 1))
    band = np.arange(P) % (P // C)
    top, bottom = (band > 0).astype(np.float64), (band < P // C - 1).astype(np.float64)
    halo = np.stack([top, BORDER * (1 - top), bottom, BORDER * (1 - bottom)], axis=1)
    taps = np.zeros((16, 9, 9, 16))
    for p in range(16):
        for t in range(9):
            for m in range(16):
                kh = 4 * (t // 3 - 1) + p // 4 - m // 4 + 1
                kw = 4 * (t % 3 - 1) + p % 4 - m % 4 + 1
                if 0 <= kh < 3 and 0 <= kw < 3:
                    taps[p, 3 * kh + kw, t, m] = 1
    said = {
        "center": np.eye(P) - 1 / P, "mean": np.full((P, P), 1 / P), "ident": np.eye(P), "group": group,
        "halo": halo, "select": select, "taps": np.tile(taps.reshape(16, -1), (C, 1)),
    }
    return {k: v.astype(np.float32) for k, v in said.items()}


def kernel(x, L1_conv_ln_gamma, L1_conv_ln_beta, L1_conv_in_proj_w, L1_conv_conv_w, L1_conv_conv_b,
           L1_conv_x_proj_w, L1_conv_dt_proj_w, L1_conv_dt_proj_b, L1_conv_A_log, L1_conv_D,
           L1_conv_out_proj_w, L2_conv_weight, L2_conv_bias, L3_conv_weight, L3_conv_bias):
    import numpy as np
    import concourse.bacc as bacc
    from concourse.bass_utils import run_bass_kernel_spmd

    def column(a):
        return np.asarray(a).reshape(-1, 1)

    xp = np.asarray(L1_conv_x_proj_w)
    scan_w = {
        "in_x_t": np.asarray(L1_conv_in_proj_w)[:DI].T, "in_z_t": np.asarray(L1_conv_in_proj_w)[DI:].T,
        "x_proj_t": np.concatenate([xp[DTR:], xp[:DTR]]).T,
        "out_proj_t": np.asarray(L1_conv_out_proj_w).T, "dt_proj_t": np.asarray(L1_conv_dt_proj_w).T,
        "conv_w_t": np.asarray(L1_conv_conv_w).reshape(DI, TAPS).T, "conv_b": column(L1_conv_conv_b),
        "dt_b": column(L1_conv_dt_proj_b), "d": column(L1_conv_D), "a_log": np.asarray(L1_conv_A_log),
        "gamma": column(L1_conv_ln_gamma), "beta": column(L1_conv_ln_beta),
    }
    convs = {}
    for n, (w, bias) in enumerate(((L2_conv_weight, L2_conv_bias), (L3_conv_weight, L3_conv_bias))):
        by_tap = np.asarray(w).reshape(C, C, 9).transpose(1, 2, 0).reshape(C, 72)
        convs[f"w{n}"] = np.repeat(by_tap, R * R, axis=0)
        convs[f"b{n}"] = np.repeat(column(bias), R * R, axis=0)

    nc = bacc.Bacc("TRN2", target_bir_lowering=False, num_devices=1)
    arrays = {}

    def give(name, a):
        a = np.ascontiguousarray(a)
        arrays[name] = a
        return nc.dram_tensor(name, a.shape, mybir.dt.from_np(a.dtype), kind="ExternalInput").ap()

    x_in = give("x", x)
    scan_in = {k: give(f"mamba_{k}", v) for k, v in scan_w.items()}
    conv_in = {k: give(f"conv_{k}", v) for k, v in convs.items()}
    table_in = {k: give(f"table_{k}", v) for k, v in tables().items()}
    out = nc.dram_tensor("out", (B, C, H, W), F32, kind="ExternalOutput").ap()
    build(nc, x_in, scan_in, [conv_in["w0"], conv_in["w1"]], [conv_in["b0"], conv_in["b1"]], table_in, out)
    return run_bass_kernel_spmd(nc, [arrays], core_ids=[0]).results[0]["out"]
```

```python
from contextlib import ExitStack

import concourse.bass as bass
from concourse import mybir

F32 = mybir.dt.float32
BF16 = mybir.dt.bfloat16
ALU = mybir.AluOpType
ACT = mybir.ActivationFunctionType

P = 128
B, C, H, W = 16, 8, 256, 256
R = 4
TH, TW = H // R, W // R
L = TH * TW
BAND = H // (P // C)
NB = H // BAND
BANDS = BAND // R
T = 512
NC = L // T
TROWS = T // TW
CB = T // W
DI = 256
NH = DI // P
S = 32
DTR = 8
TAPS = 4
PAD = TAPS - 1
XR = 2 * S + DTR
ER = 2 * 3 * C
BORDER = -2.0
EPS = 1e-5
RING = 2
LAG = 3
GS = 5
LOG_EXP = "natural_log_exp_and_others"

CENTER, VAR, OUT, XPROJ = 0, 2, 4, 19
X_AT, Z_AT, DT_AT = (6, 9), (12, 14), (22, 24)
BLOCKS = (16, 26, 29)
CONV_AT = {}
for n, places in enumerate((((1, 0), (1, 1), (1, 2), (2, 0), (2, 1), (2, 2), (3, 0), (3, 1)),
                            ((4, 1), (4, 2), (5, 0), (5, 1), (5, 2), (6, 0), (7, 0), (7, 1)))):
    for k, (c, place) in enumerate(places):
        CONV_AT[n, k] = (c, BLOCKS[place])
MEAN_AT = {"joint": (0, 26), "z1": (3, 29), "x1": (6, 26)}
VAR_AT = {"joint": (0, 28), "z1": (4, 16), "x1": (6, 28)}
DIL_SLOTS = (1, 4, 8, 12, 15, 19, 22)
PADDED_AT = ((0, 31), (4, 19))
RAW_STATS, Z_STATS, X1_STATS = (0, 6), (0, 18), (6, 18)
BASE, X1_LOAD = 8, (6, 9)

RAW, Z0, Z1, X1 = range(4)
NORMS = {"raw_first": (RAW, RAW + 1), "x1_first": (X1, X1 + 1), "joint": (RAW, Z0 + 1), "z1": (Z1, Z1 + 1),
         "x1": (X1, X1 + 1), "z0_last": (Z0, Z0 + 1), "z1_last": (Z1, Z1 + 1)}


def tensor_extras(c, s):
    work = []
    for name, at in (("center", CENTER), ("var", VAR), ("xproj", XPROJ)):
        if s == at:
            work.append((1, (name, c)))
    if s == OUT and c > 0:
        work.append((1, ("out", c - 1)))
    for half in range(NH):
        if s in (X_AT[half], X_AT[half] + 1):
            work.append((s - X_AT[half], ("x", c, half)))
        if s == Z_AT[half]:
            work.append((1, ("z", c, half)))
        if s == DT_AT[half]:
            work.append((1, ("dt", c, half)))
    for (n, k), (at_c, at_s) in CONV_AT.items():
        if at_c == c and s in (at_s, at_s + 1):
            work.append((s - at_s, ("conv", n, k)))
    for name in MEAN_AT:
        if MEAN_AT[name] == (c, s):
            work.append((1, ("gn_mean", name)))
        if VAR_AT[name] == (c, s):
            work.append((1, ("gn_var", name)))
    return work


FIRST_USES = [("gn_mean", "raw_first"), ("gn_var", "raw_first"), ("gn_mean", "x1_first"), ("gn_var", "x1_first"),
              ("center", -1), ("var", -1), ("x", -1, 0), ("x", -1, 1), ("z", -1, 0), ("z", -1, 1), ("xproj", -1),
              ("dt", -1, 0), ("dt", -1, 1)]
USES = [use for c in range(NC) for s in range(S) for part, use in tensor_extras(c, s) if part] + [("out", NC - 1)]
LAST_USES = ([("gn_mean", "z0_last"), ("gn_var", "z0_last")] + [("conv_last", 0, k) for k in range(NC)]
             + [("gn_mean", "z1_last"), ("gn_var", "z1_last")] + [("conv_last", 1, k) for k in range(NC)])


def build(nc, x, scan_w, conv_w, const, out):
    x1_dram = nc.dram_tensor("x1_dram", (C, TH, R, R, TW), F32, kind="Internal").ap()
    x2_dram = nc.dram_tensor("x2_dram", (TH, P, TW), F32, kind="Internal").ap()
    with ExitStack() as ctx:
        def sb(name, shape, dt=F32):
            return ctx.enter_context(nc.sbuf_tensor(name, shape, dt))

        def ps(name, shape):
            return ctx.enter_context(nc.psum_tensor(name, shape, F32))

        def sem(name):
            return ctx.enter_context(nc.semaphore(name))

        center_m = sb("center_m", [P, P])
        mean_m = sb("mean_m", [P, P])
        ident = sb("ident", [P, P])
        group_m = sb("group_m", [P, P])
        group_z = sb("group_z", [P, P])
        halo_keep = sb("halo_keep", [P, 4])
        select = sb("select", [3 * S, S * P], BF16)
        w_x = sb("w_x", [P, TAPS, DI])
        w_z = sb("w_z", [P, DI])
        w_xp = sb("w_xp", [P, NH, XR])
        w_dt = sb("w_dt", [2 * S + DTR, DI])
        w_out = sb("w_out", [P, NH, P])
        conv_bias = sb("conv_bias", [P, NH])
        dt_bias = sb("dt_bias", [P, NH])
        d_skip = sb("d_skip", [P, NH])
        a_neg = sb("a_neg", [P, NH * S])
        gamma = sb("gamma", [P, 1])
        beta = sb("beta", [P, 1])
        w_main = [sb(f"w_main{n}", [P, 3, P]) for n in range(2)]
        w_edge = [sb(f"w_edge{n}", [ER + 1, P]) for n in range(2)]
        eps_col = sb("eps_col", [P, 1])

        raw = sb("raw", [P, BAND + 2, W])
        norm = sb("norm", [P, R + 2, W + 2])
        vmax = sb("vmax", [P, R, W + 2])
        x1 = sb("x1", [P, L])
        z = sb("z", [P, L])
        padded = sb("padded", [P, NB + 2, W + 2])
        edge = sb("edge", [2 * S, 2, T])
        stats = sb("stats", [P, 4, NC, 6])
        mv = sb("mv", [P, 4, 2])
        g_mean = sb("g_mean", [P, 4])
        g_dev = sb("g_dev", [P, 4])
        g_var = sb("g_var", [P, 4])
        g_log = sb("g_log", [P, 4])
        g_rstd = sb("g_rstd", [P, 4])
        g_shift = sb("g_shift", [P, 4])
        halo = sb("halo", [P, 4])
        spare = sb("spare", [P, 1])

        g1 = sb("g1", [P, T])
        x2 = sb("x2", [P, 2, T])
        u_ln = sb("u_ln", [P, PAD + T])
        cen = sb("cen", [P, T])
        sq = sb("sq", [P, T])
        rstd = sb("rstd", [P, T])
        xz = sb("xz", [P, 2, NH, T])
        xc = sb("xc", [P, 2, NH, T])
        zs = sb("zs", [P, 2, NH, T])
        dt = sb("dt", [P, 2, NH, T])
        dtx = sb("dtx", [P, 2, NH, T])
        rest = sq[0:2 * S, :]
        parts = sb("parts", [2 * S, 3, T], BF16)
        dt_rows = cen
        b_parts = sb("b_parts", [3 * S, 2, T], BF16)
        c_parts = sb("c_parts", [3 * S, 2, T], BF16)
        u_in = sb("u_in", [P, RING, NH, T])
        h = sb("h", [P, RING, NH, T])
        hc = sb("hc", [P, RING, NH, T])
        c_sb = sb("c_sb", [P, RING, T])
        carry = sb("carry", [P, NH, S])

        scratch = ps("scratch", [P, T])
        b_ps = ps("b_ps", [P, 2, T])
        c_ps = ps("c_ps", [P, T])
        a_ps = ps("a_ps", [P, NH, T])
        y_ps = ps("y_ps", [P, NH, T])

        weights_in = sem("weights_in")
        edge_zero = sem("edge_weights_zero")
        select_in = sem("select_in")
        setup_v = sem("setup_v")
        setup_a = sem("setup_a")
        setup_p = sem("setup_p")
        filled = sem("scratch_filled")
        emptied = sem("scratch_emptied")
        raw_in = sem("raw_in")
        dil = sem("dilation_steps")
        x1_rows_out = sem("x1_rows_out")
        x1_in = sem("x1_patch_in")
        st = sem("group_stats")
        gs = sem("group_norm_steps")
        ga = sem("group_rstd")
        g1_done = sem("g1_done")
        base_done = sem("x1_plus_g1")
        x2_out = sem("x2_chunk_out")
        z_in = sem("z_in")
        padded_done = sem("padded_done")
        edge_in = [sem(f"edge_rows_in{k}") for k in range(2)]
        stored = sem("stored")
        carry_u = sem("u_tail_kept")
        rstd_done = sem("rstd_done")
        scaled = sem("token_scaled")
        u_done = sem("u_ln_done")
        silu_done = sem("silu_done")
        hi_done = sem("part_hi")
        mid_done = sem("part_mid")
        lo_done = sem("part_lo")
        parts_in = sem("parts_moved")
        exp_done = sem("dt_exp")
        ln_done = sem("dt_ln")
        dt_done = sem("dt_done")
        dtx_done = sem("dtx_done")
        b_cast = sem("b_broadcast")
        c_cast = sem("c_broadcast")
        u_made = sem("state_input")
        a_made = sem("decay")
        c_copied = sem("c_copied")
        h_done = sem("h_done")
        kept = sem("carry_kept")
        hc_done = sem("hc_done")
        summed = sem("y_summed")
        skip_done = sem("y_plus_skip")
        gated = sem("y_gated")

        block = ctx.enter_context(nc.Block())

        def used(b, *use):
            if use in FIRST_USES:
                return FIRST_USES.index(use) + 1
            if use in LAST_USES:
                return len(FIRST_USES) + B * len(USES) + LAST_USES.index(use) + 1
            return b * len(USES) + len(FIRST_USES) + USES.index(use) + 1

        def read(b, *use):
            return used(b, *use) + 1

        def norm_number(b, name):
            if name in ("raw_first", "x1_first"):
                return ("raw_first", "x1_first").index(name)
            if name in ("z0_last", "z1_last"):
                return 2 + 3 * B + ("z0_last", "z1_last").index(name)
            return b * 3 + 2 + ("joint", "z1", "x1").index(name)

        def chunk(b, c, n=1):
            return (b * NC + (c + 1)) * n

        def state(b, c, s, n=1):
            return (b * (NC * S) + (c * S + s + 1 + RING)) * n

        def start_ahead(engine, *semaphores, n=1):
            for semaphore in semaphores:
                engine.sem_inc(semaphore, RING * n)

        def kept_state(b, c, s):
            return b * ((NC - 1) * S) + (c * S + s + 1)

        def behind(c, s, n):
            at = c * S + s - n
            return at // S, at % S

        N_WEIGHTS = 33
        SETUP_V = 4 + TAPS + 2 * (9 + 6)
        SETUP_P = 4
        DIL_AT = [4 + 6 * (k + 1) + 1 + (k == BANDS - 1) for k in range(BANDS)]
        DIL = DIL_AT[-1]

        @block.sync
        def _(sp):
            def load(dst, src):
                sp.dma_start(dst, src).then_inc(weights_in, 16)

            load(center_m[:, :], const["center"])
            load(mean_m[:, :], const["mean"])
            load(ident[:, :], const["ident"])
            load(group_m[:, :], const["group"])
            load(group_z[:, :], const["group_z"])
            load(halo_keep[:, :], const["halo"])
            load(w_x[:, 0, :], scan_w["in_x_t"])
            load(w_z[:, :], scan_w["in_z_t"])
            for half in range(NH):
                rows = slice(half * P, (half + 1) * P)
                load(w_xp[:, half, :], scan_w["x_proj_t"][rows, :])
                load(w_out[:, half, :], scan_w["out_proj_t"][rows, :])
                load(conv_bias[:, half:half + 1], scan_w["conv_b"][rows, :])
                load(dt_bias[:, half:half + 1], scan_w["dt_b"][rows, :])
                load(d_skip[:, half:half + 1], scan_w["d"][rows, :])
                load(a_neg[:, half * S:(half + 1) * S], scan_w["a_log"][rows, :])
            load(w_dt[2 * S:, :], scan_w["dt_proj_t"])
            load(gamma[:, :], scan_w["gamma"])
            load(beta[:, :], scan_w["beta"])
            load(norm[:, 0:TAPS, 0:DI], scan_w["conv_w_t"].partition_broadcast(P))
            load(sq[:, 144:192], const["taps"])
            for n in range(2):
                load(sq[:, 72 * n:72 * (n + 1)], conv_w[f"main{n}"])
            sp.wait_ge(edge_zero, 2)
            for n in range(2):
                with nc.allow_non_contiguous_dma(reason="a few weights, once"):
                    load(w_edge[n][0:ER // 2, 0:C * R:R], conv_w[f"above{n}"])
                    load(w_edge[n][ER // 2:ER, P - C * R + R - 1:P:R], conv_w[f"below{n}"])
                load(w_edge[n][ER:ER + 1, :], conv_w[f"bias{n}"])
            sp.dma_start(x1[0:3 * S, :], const["select"]).then_inc(select_in, 16)

            def load_raw(image):
                img = x[bass.ds(image, 1)].rearrange("o c (g r) w -> (o c g) (r w)", r=BAND)
                sp.dma_start(raw[:, 1:BAND + 1, :], img).then_inc(raw_in, 16)
                sp.dma_start(raw[1:P, 0:1, :], img[0:P - 1, (BAND - 1) * W:]).then_inc(raw_in, 16)
                sp.dma_start(raw[0:P - 1, BAND + 1:, :], img[1:P, 0:W]).then_inc(raw_in, 16)

            def store_x1_rows(number, k):
                sp.wait_ge(dil, number * DIL + DIL_AT[k])
                sp.dma_start(x1_dram.rearrange("c (g l) r q w -> l (c g) r (q w)", l=BANDS)[k],
                             vmax[:, :, 0:W]).then_inc(x1_rows_out, 16)

            def load_x1(number):
                sp.wait_ge(x1_rows_out, number * (BANDS * 16) + BANDS * 16)
                for ch in range(C):
                    sp.dma_start(x1[ch * R * R:(ch + 1) * R * R, :].rearrange("p (t w) -> p t w", w=TW),
                                 x1_dram[ch].rearrange("t r q w -> (r q) t w")).then_inc(x1_in, 16)

            def move_parts(b, c):
                sp.wait_ge(lo_done, chunk(b, c + 1))
                for k in range(3):
                    for rows, to in ((slice(0, S), b_parts), (slice(S, 2 * S), c_parts)):
                        sp.dma_start(to[k * S:(k + 1) * S, (c + 1) % 2, :], parts[rows, k, :]).then_inc(parts_in, 16)

            def store_x2(b, c):
                sp.wait_ge(emptied, read(b, "out", c))
                if c == 0:
                    sp.wait_ge(z_in, b * (BANDS * 16) + BANDS * 16)
                sp.dma_start(x2_dram[c * TROWS:(c + 1) * TROWS].rearrange("t p w -> p t w"),
                             x2[:, c % 2].rearrange("p (t w) -> p t w", w=TW)).then_inc(x2_out, 16)

            def load_z(b):
                sp.wait_ge(x2_out, b * (NC * 16) + 16)
                for k in range(BANDS):
                    sp.dma_start(z[k * C * R:(k + 1) * C * R, :].rearrange("p (g w) -> p g w", g=NB),
                                 z_source(k)).then_inc(z_in, 16)

            def z_source(k):
                return x2_dram.rearrange("t p w -> t (p w)").rearrange("(g l) (m v) -> l m g v", l=BANDS, v=W)[k]

            def load_edge(b, n, k, conv="conv"):
                if k < 2:
                    sp.wait_ge(padded_done, b * 2 + n + 1)
                else:
                    sp.wait_ge(filled, used(b, conv, n, k - 2))
                for dw in range(3):
                    sp.dma_start(edge[dw * C:(dw + 1) * C, k % 2, :].rearrange("p (g w) -> p g w", w=W),
                                 padded[P - C * R + R - 1:P:R, CB * k:CB * (k + 1), dw:dw + W]).then_inc(edge_in[k % 2], 16)
                    sp.dma_start(edge[(3 + dw) * C:(4 + dw) * C, k % 2, :].rearrange("p (g w) -> p g w", w=W),
                                 padded[0:C * R:R, CB * k + 2:CB * (k + 1) + 2, dw:dw + W]).then_inc(edge_in[k % 2], 16)

            def store_output(b, image, conv="conv"):
                sp.wait_ge(emptied, read(b, conv, 1, NC - 1))
                for k in range(BANDS):
                    for r in range(R):
                        rows = raw[k * C * R + r:(k + 1) * C * R:R, 1:BAND + 1, :]
                        sp.dma_start(out_rows(image, k * R + r), rows).then_inc(stored, 16)

            def out_rows(image, r):
                return out[bass.ds(image, 1)].rearrange("o c (g r) w -> r (o c) g w", r=BAND)[r]

            sp.wait_ge(setup_p, SETUP_P)
            sp.wait_ge(setup_v, SETUP_V)
            sp.dma_start(x2_dram.rearrange("t p w -> p t w"),
                         z[:, :].rearrange("p (t w) -> p t w", w=TW)).then_inc(x2_out, 16)
            load_raw(0)
            for k in range(BANDS):
                store_x1_rows(0, k)
            sp.wait_ge(setup_a, 2)
            load_x1(0)
            move_parts(0, -1)
            sp.sem_inc(stored, BAND * 16)
            with sp.Fori(0, B) as b:
                image_ahead, image_behind = sp.snap((b + 1) % B), sp.snap((b + (B - 1)) % B)
                for c in range(NC):
                    for s in range(S):
                        if (c, s) == (0, 0):
                            sp.wait_ge(stored, b * (BAND * 16) + BAND * 16)
                            load_raw(image_ahead)
                            load_z(b)
                        if s == OUT + 2 and c > 0:
                            store_x2(b, c - 1)
                        if s == 24:
                            move_parts(b, c)
                        if s == DIL_SLOTS[-1] and 1 <= c <= BANDS:
                            store_x1_rows(b + 1, c - 1)
                        if (c, s) == X1_LOAD:
                            sp.wait_ge(base_done, chunk(b, NC - 1))
                            load_x1(b + 1)
                        for n in range(2):
                            if (c, s) == PADDED_AT[n]:
                                load_edge(b, n, 0)
                                load_edge(b, n, 1)
                            for k in range(2, NC):
                                if CONV_AT[n, k - 2] == (c, s - 1):
                                    load_edge(b, n, k)
                        if CONV_AT[1, NC - 1] == (c, s - 2):
                            store_output(b, image_behind)
                store_x2(b, NC - 1)
            sp.wait_ge(stored, (B + 1) * BAND * 16)
            load_z(B)
            for n in range(2):
                for k in range(NC):
                    load_edge(B, n, k, "conv_last")
            store_output(B, B - 1, "conv_last")
            sp.wait_ge(stored, (B + 2) * BAND * 16)

        @block.gpsimd
        def _(pool):
            pool.memset(w_edge[0][:, :], 0.0).then_inc(edge_zero, 1)
            pool.memset(w_edge[1][:, :], 0.0).then_inc(edge_zero, 1)
            pool.memset(raw[:, :, :], 0.0).then_inc(setup_p, 1)
            pool.memset(padded[:, :, :], 0.0).then_inc(setup_p, 1)
            pool.memset(edge[:, :, :], 1.0).then_inc(setup_p, 1)
            pool.memset(z[:, :], 0.0).then_inc(setup_p, 1)

            def scale_tokens(b, c):
                pool.wait_ge(rstd_done, chunk(b, c + 1))
                pool.tensor_tensor(cen[:, :], cen[:, :], rstd[:, :], ALU.mult).then_inc(scaled, 1)

            def make_base(b, c):
                pool.wait_ge(g1_done, chunk(b, c + 1))
                pool.wait_ge(x2_out, chunk(b, c, 16))
                at = (c + 1) % NC
                pool.tensor_tensor(x2[:, at % 2], x1[:, at * T:(at + 1) * T], g1[:, :], ALU.add).then_inc(base_done, 1)

            pool.wait_ge(g1_done, 1)
            pool.tensor_tensor(x2[:, 0], x1[:, 0:T], g1[:, :], ALU.add).then_inc(base_done, 1)
            scale_tokens(0, -1)
            start_ahead(pool, hc_done)
            with pool.Fori(0, B) as b:
                for c in range(NC):
                    for s in range(S):
                        r = s % RING
                        pool.wait_ge(c_copied, state(b, c, s))
                        pool.wait_ge(h_done, state(b, c, s, NH))
                        pool.wait_ge(summed, state(b, *behind(c, s, RING)))
                        pool.tensor_tensor(hc[:, r], h[:, r], c_sb[:, r:r + 1, :].broadcast_to([P, NH, T]),
                                           ALU.mult).then_inc(hc_done, 1)
                        if s == VAR + 1:
                            scale_tokens(b, c)
                        if s == BASE:
                            make_base(b, c)

        @block.scalar
        def _(act):
            act.preload_act_table_set(LOG_EXP)
            act.wait_ge(weights_in, N_WEIGHTS * 16)
            act.activation(a_neg[:, :], a_neg[:, :], ACT.Exp).then_inc(setup_a, 1)
            act.wait_ge(select_in, 16)
            act.activation(select[:, :], x1[0:3 * S, :], ACT.Copy).then_inc(setup_a, 1)
            act.wait_ge(setup_v, 1)

            def group_rstd(b, name):
                lo, hi = NORMS[name]
                act.wait_ge(filled, used(b, "gn_var", name))
                act.activation(g_log[:, lo:hi], scratch[:, 0:hi - lo], ACT.Ln, bias=eps_col[:, :]).then_inc(emptied, 1)
                act.wait_ge(emptied, read(b, "gn_var", name))
                act.activation(g_rstd[:, lo:hi], g_log[:, lo:hi], ACT.Exp, scale=-0.5).then_inc(ga, 1)

            def centered(b, c):
                act.wait_ge(filled, used(b, "center", c))
                act.activation(cen[:, :], scratch[:, :], ACT.Copy)
                act.activation(sq[:, :], scratch[:, :], ACT.Square).then_inc(emptied, 1)

            def token_rstd(b, c):
                act.wait_ge(filled, used(b, "var", c))
                act.activation(rstd[:, :], scratch[:, :], ACT.Ln, bias=eps_col[:, :]).then_inc(emptied, 1)
                act.wait_ge(emptied, read(b, "var", c))
                act.activation(rstd[:, :], rstd[:, :], ACT.Exp, scale=-0.5).then_inc(rstd_done, 1)

            def layer_norm(b, c):
                if (c + 1) % NC:
                    act.activation(u_ln[:, 0:PAD], u_ln[:, T:T + PAD], ACT.Copy).then_inc(carry_u, 1)
                else:
                    act.memzero(u_ln[:, 0:PAD]).then_inc(carry_u, 1)
                act.wait_ge(carry_u, chunk(b, c + 1))
                act.wait_ge(scaled, chunk(b, c + 1))
                act.activation(u_ln[:, PAD:], cen[:, :], ACT.Identity, bias=beta[:, :],
                               scale=gamma[:, :]).then_inc(u_done, 1)

            def copy_x(b, c, half):
                act.wait_ge(filled, used(b, "x", c, half))
                act.activation(xz[:, 0, half], scratch[:, :], ACT.Identity,
                               bias=conv_bias[:, half:half + 1]).then_inc(emptied, 1)

            def copy_z(b, c, half):
                act.wait_ge(filled, used(b, "z", c, half))
                act.activation(xz[:, 1, half], scratch[:, :], ACT.Copy).then_inc(emptied, 1)

            def silus(b, c):
                act.wait_ge(emptied, read(b, "z", c, NH - 1))
                act.activation(xc[:, (c + 1) % 2], xz[:, 0], ACT.Silu)
                act.activation(zs[:, (c + 1) % 2], xz[:, 1], ACT.Silu).then_inc(silu_done, 1)
                act.preload_act_table_set(LOG_EXP)

            def split_hi(b, c):
                act.wait_ge(filled, used(b, "xproj", c))
                act.activation(dt_rows[2 * S:XR, :], scratch[2 * S:XR, :], ACT.Copy)
                act.activation(parts[:, 0, :], scratch[0:2 * S, :], ACT.Copy).then_inc(hi_done, 1)

            def split_mid(b, c):
                act.wait_ge(emptied, read(b, "xproj", c))
                act.activation(parts[:, 1, :], rest[:, :], ACT.Copy).then_inc(mid_done, 1)

            def softplus_in(b, c, half):
                act.wait_ge(filled, used(b, "dt", c, half))
                act.activation(xz[:, 0, half], scratch[:, :], ACT.Abs, bias=dt_bias[:, half:half + 1])
                act.activation(xz[:, 1, half], scratch[:, :], ACT.Relu,
                               bias=dt_bias[:, half:half + 1]).then_inc(emptied, 1)

            def softplus_log(b, c):
                act.wait_ge(emptied, read(b, "dt", c, NH - 1))
                act.activation(xz[:, 0], xz[:, 0], ACT.Exp, scale=-1.0).then_inc(exp_done, 1)
                act.wait_ge(exp_done, chunk(b, c + 1))
                act.activation(xz[:, 0], xz[:, 0], ACT.Ln, bias=1.0).then_inc(ln_done, 1)

            def keep(b, c, s):
                act.wait_ge(h_done, state(b, c, s, NH))
                act.activation(carry[:, :, s:s + 1], h[:, s % RING, :, T - 1:T], ACT.Copy).then_inc(kept, 1)

            group_rstd(0, "raw_first")
            group_rstd(0, "x1_first")
            centered(0, -1)
            token_rstd(0, -1)
            layer_norm(0, -1)
            for half in range(NH):
                copy_x(0, -1, half)
            for half in range(NH):
                copy_z(0, -1, half)
            silus(0, -1)
            split_hi(0, -1)
            split_mid(0, -1)
            softplus_in(0, -1, 0)
            softplus_in(0, -1, 1)
            softplus_log(0, -1)
            start_ahead(act, c_copied)
            start_ahead(act, a_made, n=NH)
            with act.Fori(0, B) as b:
                for c in range(NC):
                    act.wait_ge(dt_done, chunk(b, c))
                    for s in range(S):
                        r = s % RING
                        for half in range(NH):
                            act.wait_ge(h_done, state(b, *behind(c, s, 1), NH) - (NH - 1 - half))
                            at = half * S + s
                            act.activation(a_ps[:, half], dt[:, c % 2, half], ACT.Exp,
                                           scale=a_neg[:, at:at + 1]).then_inc(a_made, 1)
                        act.wait_ge(c_cast, state(b, c, s))
                        act.wait_ge(hc_done, state(b, *behind(c, s, RING)))
                        act.activation(c_sb[:, r], c_ps[:, :], ACT.Copy).then_inc(c_copied, 1)
                        if (c or s) and (c < NC - 1 or s == 0):
                            keep(b, *behind(c, s, 1))
                        if s == CENTER + 1:
                            centered(b, c)
                        if s == VAR + 1:
                            token_rstd(b, c)
                        if s == VAR + 2:
                            layer_norm(b, c)
                        for half in range(NH):
                            if s == X_AT[half] + 2:
                                copy_x(b, c, half)
                            if s == Z_AT[half] + 1:
                                copy_z(b, c, half)
                            if s == DT_AT[half] + 1:
                                softplus_in(b, c, half)
                        if s == Z_AT[-1] + 1:
                            silus(b, c)
                        if s == XPROJ + 1:
                            split_hi(b, c)
                        if s == XPROJ + 3:
                            split_mid(b, c)
                        if s == DT_AT[-1] + 1:
                            softplus_log(b, c)
                        for name in VAR_AT:
                            if VAR_AT[name] == (c, s - 1):
                                group_rstd(b, name)
            group_rstd(B, "z0_last")
            group_rstd(B, "z1_last")

        @block.tensor
        def _(pe):
            pe.wait_ge(weights_in, N_WEIGHTS * 16)
            pe.wait_ge(setup_v, SETUP_V)
            pe.wait_ge(setup_a, 2)
            pe.wait_ge(setup_p, SETUP_P)

            def take_scratch(b, *use):
                pe.wait_ge(emptied, used(b, *use))

            def group_product(b, name, rhs):
                lo, hi = NORMS[name]
                for n in range(lo, hi):
                    mm = pe.matmul(scratch[:, n - lo:n - lo + 1], (group_z if n in (Z0, Z1) else group_m)[:, :],
                                   rhs(n), start=True, stop=True, skip_group_check=True)
                mm.then_inc(filled, 1)

            def group_mean(b, name):
                pe.wait_ge(gs, norm_number(b, name) * GS + 1)
                take_scratch(b, "gn_mean", name)
                group_product(b, name, lambda n: mv[:, n, 0:1])

            def group_var(b, name):
                pe.wait_ge(gs, norm_number(b, name) * GS + 4)
                take_scratch(b, "gn_var", name)
                group_product(b, name, lambda n: g_var[:, n:n + 1])

            def center(b, c):
                pe.wait_ge(g1_done, chunk(b, c + 1))
                take_scratch(b, "center", c)
                pe.matmul(scratch[:, :], center_m[:, :], g1[:, :], start=True, stop=True).then_inc(filled, 1)

            def variance(b, c):
                take_scratch(b, "var", c)
                pe.matmul(scratch[:, :], mean_m[:, :], sq[:, :], start=True, stop=True).then_inc(filled, 1)

            def project_x(b, c, half, part):
                if part == 0:
                    pe.wait_ge(u_done, chunk(b, c + 1))
                    take_scratch(b, "x", c, half)
                for k in range(part * TAPS // 2, (part + 1) * TAPS // 2):
                    mm = pe.matmul(scratch[:, :], w_x[:, k, half * P:(half + 1) * P], u_ln[:, k:k + T],
                                   start=(k == 0), stop=(k == TAPS - 1), skip_group_check=True)
                if part:
                    mm.then_inc(filled, 1)

            def project_z(b, c, half):
                take_scratch(b, "z", c, half)
                pe.matmul(scratch[:, :], w_z[:, half * P:(half + 1) * P], u_ln[:, PAD:],
                          start=True, stop=True).then_inc(filled, 1)

            def x_proj(b, c):
                pe.wait_ge(silu_done, chunk(b, c + 1))
                take_scratch(b, "xproj", c)
                for half in range(NH):
                    mm = pe.matmul(scratch[0:XR, :], w_xp[:, half, :], xc[:, (c + 1) % 2, half],
                                   start=(half == 0), stop=(half == NH - 1))
                mm.then_inc(filled, 1)

            def dt_proj(b, c, half):
                pe.wait_ge(hi_done, chunk(b, c + 1))
                take_scratch(b, "dt", c, half)
                pe.matmul(scratch[:, :], w_dt[2 * S:XR, half * P:(half + 1) * P], dt_rows[2 * S:XR, :],
                          start=True, stop=True).then_inc(filled, 1)

            def out_proj(b, c):
                pe.wait_ge(gated, chunk(b, c))
                take_scratch(b, "out", c)
                for half in range(NH):
                    mm = pe.matmul(scratch[:, :], w_out[:, half, :], xc[:, c % 2, half],
                                   start=(half == 0), stop=(half == NH - 1))
                mm.then_inc(filled, 1)

            def sum_states(b, c, s):
                pe.wait_ge(hc_done, state(b, c, s))
                if s == 0 and c:
                    pe.wait_ge(skip_done, chunk(b, c - 1, NH))
                for half in range(NH):
                    mm = pe.matmul(y_ps[:, half], ident[:, :], hc[:, s % RING, half],
                                   start=(s == 0), stop=(s == S - 1), skip_group_check=True)
                mm.then_inc(summed, 1)

            def convolve(b, use, part):
                _, n, k = use
                out_rows = scratch[:, :].rearrange("p (g w) -> p g w", w=W)
                if part == 0:
                    pe.wait_ge(padded_done, b * 2 + n + 1)
                    take_scratch(b, *use)
                for dw in ((0, 1), (2,))[part]:
                    pe.matmul(out_rows, w_main[n][:, dw, :], padded[:, 1 + CB * k:1 + CB * (k + 1), dw:dw + W],
                              start=(dw == 0), stop=False, skip_group_check=True)
                if part:
                    pe.wait_ge(edge_in[k % 2], b * (NC * 6 * 16) + ((n * NC + k) // 2 + 1) * (6 * 16))
                    pe.matmul(scratch[:, :], w_edge[n][:, :], edge[0:ER + 1, k % 2, :],
                              start=False, stop=True, skip_group_check=True).then_inc(filled, 1)

            def extra(b, part, use):
                name, *at = use
                if name == "conv":
                    convolve(b, use, part)
                elif name == "x":
                    project_x(b, *at, part)
                else:
                    {"center": center, "var": variance, "z": project_z, "xproj": x_proj, "dt": dt_proj,
                     "out": out_proj, "gn_mean": group_mean, "gn_var": group_var}[name](b, *at)

            for use in FIRST_USES:
                for part in ((0, 1) if use[0] == "x" else (1,)):
                    extra(0, part, use)
            start_ahead(pe, b_cast, c_cast, summed)
            with pe.Fori(0, B) as b:
                for c in range(NC):
                    pe.wait_ge(parts_in, chunk(b, c, 6 * 16))
                    for s in range(S):
                        sel = select[:, s * P:(s + 1) * P]
                        pe.wait_ge(u_made, state(b, *behind(c, s, 2)))
                        pe.matmul(b_ps[:, s % 2], sel, b_parts[:, c % 2, :], start=True, stop=True).then_inc(b_cast, 1)
                        pe.wait_ge(c_copied, state(b, *behind(c, s, 1)))
                        pe.matmul(c_ps[:, :], sel, c_parts[:, c % 2, :], start=True, stop=True).then_inc(c_cast, 1)
                        if c or s >= LAG:
                            sum_states(b, *behind(c, s, LAG))
                        for part, use in tensor_extras(c, s):
                            extra(b, part, use)
                for s in range(S - LAG, S):
                    sum_states(b, NC - 1, s)
                out_proj(b, NC - 1)
            for use in LAST_USES:
                if use[0] == "conv_last":
                    convolve(B, use, 0)
                    convolve(B, use, 1)
                else:
                    extra(B, 1, use)

        @block.vector
        def _(dve):
            steps = 0

            def own(ins):
                nonlocal steps
                steps += 1
                ins.then_inc(setup_v, 1)
                dve.wait_ge(setup_v, steps)

            own(dve.memset(eps_col[:, :], EPS))
            dve.wait_ge(weights_in, N_WEIGHTS * 16)
            dve.wait_ge(setup_a, 1)
            own(dve.tensor_scalar(a_neg[:, :], a_neg[:, :], -1.0, None, ALU.mult))
            for k in reversed(range(TAPS)):
                own(dve.tensor_tensor(w_x[:, k, :], w_x[:, 0, :], norm[:, k, 0:DI], ALU.mult))
            own(dve.memset(norm[:, :, :], BORDER))
            own(dve.memset(spare[:, :], 0.0))
            for n in range(2):
                for dw in range(3):
                    for kh in range(3):
                        j = 72 * n + C * (3 * kh + dw)
                        w = sq[:, j:j + C].unsqueeze(1).unsqueeze(3)
                        at = sq[:, 144 + 16 * kh:144 + 16 * (kh + 1)].rearrange("p (l r) -> p l r", r=R).unsqueeze(2)
                        dst = cen[:, 0:P] if kh else w_main[n][:, dw, :]
                        own(dve.tensor_tensor(dst.rearrange("p (l c r) -> p l c r", l=BANDS, c=C),
                                              w.broadcast_to([P, BANDS, C, R]), at.broadcast_to([P, BANDS, C, R]),
                                              ALU.mult))
                        if kh:
                            own(dve.tensor_tensor(w_main[n][:, dw, :], w_main[n][:, dw, :], cen[:, 0:P], ALU.add))

            def partition_stats(kind, k, src):
                return dve.bn_stats(stats[:, kind, k, :], src)

            def raw_stats(k):
                return partition_stats(RAW, k, raw[:, 1 + 2 * k:3 + 2 * k, :].rearrange("p a w -> p (a w)"))

            def z_stats(kind, k):
                return partition_stats(kind, k, z[:, k * T:(k + 1) * T])

            def x1_stats(k):
                return partition_stats(X1, k, x1[:, k * T:(k + 1) * T])

            def group_local(b, name):
                lo, hi = NORMS[name]
                dve.wait_ge(st, norm_number(b, name) + 1)
                dve.memset(spare[:, :], 0.0)
                for n in range(lo, hi):
                    last = dve.bn_aggr(mv[:, n, :], stats[:, n, :, :])
                last.then_inc(gs, 1)

            def group_deviation(b, name):
                lo, hi = NORMS[name]
                at = norm_number(b, name) * GS
                dve.wait_ge(filled, used(b, "gn_mean", name))
                dve.tensor_copy(g_mean[:, lo:hi], scratch[:, 0:hi - lo]).then_inc(emptied, 1)
                dve.wait_ge(emptied, read(b, "gn_mean", name))
                dve.tensor_tensor(g_dev[:, lo:hi], mv[:, lo:hi, 0], g_mean[:, lo:hi], ALU.subtract).then_inc(gs, 1)
                dve.wait_ge(gs, at + 2)
                dve.tensor_tensor(g_dev[:, lo:hi], g_dev[:, lo:hi], g_dev[:, lo:hi], ALU.mult).then_inc(gs, 1)
                dve.wait_ge(gs, at + 3)
                dve.tensor_tensor(g_var[:, lo:hi], g_dev[:, lo:hi], mv[:, lo:hi, 1], ALU.add).then_inc(gs, 1)

            def group_shift(b, name):
                lo, hi = NORMS[name]
                dve.wait_ge(ga, norm_number(b, name) + 1)
                dve.scalar_tensor_tensor(out=g_shift[:, lo:hi], in0=g_mean[:, lo:hi], scalar=-1.0,
                                         in1=g_rstd[:, lo:hi], op0=ALU.mult, op1=ALU.mult).then_inc(gs, 1)
                dve.wait_ge(gs, norm_number(b, name) * GS + 5)

            def normed(kind, dst, src):
                return dve.tensor_scalar(dst, src, g_rstd[:, kind:kind + 1], g_shift[:, kind:kind + 1],
                                         ALU.mult, ALU.add)

            def dilation_step(number, at, ins):
                ins.then_inc(dil, 1)
                dve.wait_ge(dil, number * DIL + at)

            def halo_scales(number):
                for side in range(2):
                    keep, fill = halo_keep[:, 2 * side:2 * side + 1], halo_keep[:, 2 * side + 1:2 * side + 2]
                    dilation_step(number, 1 + 2 * side,
                                  dve.tensor_scalar(halo[:, 2 * side:2 * side + 1], keep, g_rstd[:, RAW:RAW + 1], None,
                                                    ALU.mult))
                    dilation_step(number, 2 + 2 * side,
                                  dve.scalar_tensor_tensor(out=halo[:, 2 * side + 1:2 * side + 2], in0=keep,
                                                           scalar=g_shift[:, RAW:RAW + 1], in1=fill,
                                                           op0=ALU.mult, op1=ALU.add))

            def dilate(number, k, step):
                at = 4 + 6 * k + (k > 0) + step + 1
                inner = slice(1, W + 1)
                top = norm[:, 1:R + 1, inner]
                has_halo = k in (0, BANDS - 1)
                if step == 0:
                    first, last = (1 if k == 0 else 0), (R + 1 if k == BANDS - 1 else R + 2)
                    ins = normed(RAW, norm[:, first:last, inner], raw[:, k * R + first:k * R + last, :])
                elif has_halo and step == 1:
                    side, row = (0, 0) if k == 0 else (1, R + 1)
                    ins = dve.tensor_scalar(norm[:, row:row + 1, inner], raw[:, k * R + row:k * R + row + 1, :],
                                            halo[:, 2 * side:2 * side + 1], halo[:, 2 * side + 1:2 * side + 2],
                                            ALU.mult, ALU.add)
                elif step == 1 + has_halo:
                    if k:
                        dve.wait_ge(x1_rows_out, number * (BANDS * 16) + k * 16)
                    ins = dve.tensor_tensor(vmax[:, :, :], norm[:, 0:R, :], norm[:, 1:R + 1, :], ALU.max)
                elif step == 2 + has_halo:
                    ins = dve.tensor_tensor(vmax[:, :, :], vmax[:, :, :], norm[:, 2:R + 2, :], ALU.max)
                elif step == 3 + has_halo:
                    ins = dve.tensor_tensor(top, vmax[:, :, 0:W], vmax[:, :, 1:W + 1], ALU.max)
                elif step == 4 + has_halo:
                    ins = dve.tensor_tensor(top, top, vmax[:, :, 2:W + 2], ALU.max)
                elif step == 5 + has_halo:
                    ins = dve.tensor_tensor(vmax[:, :, 0:W].rearrange("p r (q w) -> p r q w", q=R),
                                            top.rearrange("p r (w q) -> p r q w", q=R),
                                            raw[:, k * R + 1:(k + 1) * R + 1, :].rearrange("p r (w q) -> p r q w", q=R),
                                            ALU.add)
                else:
                    return
                dilation_step(number, at, ins)

            def make_g1(b, c):
                at = (c + 2) % NC
                dve.wait_ge(filled, used(b, "center", c))
                dve.wait_ge(base_done, chunk(b, c + 1))
                normed(X1, g1[:, :], x1[:, at * T:(at + 1) * T]).then_inc(g1_done, 1)

            def pad(b, n):
                normed(Z0 + n, padded[:, 1:NB + 1, 1:W + 1].rearrange("p g (w q) -> p g q w", q=R),
                       z[:, :].rearrange("p (g q w) -> p g q w", g=NB, q=R)).then_inc(padded_done, 1)

            def add_conv(b, use):
                _, n, k = use
                dve.wait_ge(filled, used(b, *use))
                block_z = z[:, k * T:(k + 1) * T].rearrange("p (g q w) -> p g q w", g=CB, q=R)
                block_o = raw[:, 1 + CB * k:1 + CB * (k + 1), :].rearrange("p g (w q) -> p g q w", q=R)
                dve.tensor_tensor(block_o if n else block_z, scratch[:, :].rearrange("p (g w q) -> p g q w", g=CB, q=R),
                                  block_z, ALU.add).then_inc(emptied, 1)
                if n == 0:
                    dve.wait_ge(emptied, read(b, *use))
                    last = z_stats(Z1, k)
                    if k == NC - 1:
                        last.then_inc(st, 1)

            def make_u(b, c, s):
                if s == 0:
                    dve.wait_ge(dtx_done, chunk(b, c))
                dve.wait_ge(b_cast, state(b, c, s))
                dve.wait_ge(h_done, state(b, *behind(c, s, RING), NH))
                dve.tensor_tensor(u_in[:, s % RING], dtx[:, c % 2],
                                  b_ps[:, s % 2:s % 2 + 1, :].broadcast_to([P, NH, T]), ALU.mult).then_inc(u_made, 1)

            def scan(b, c, s):
                r = s % RING
                dve.wait_ge(hc_done, state(b, *behind(c, s, RING)))
                if (c or s >= RING) and (c < NC - 1 or s < RING):
                    dve.wait_ge(kept, kept_state(b, *behind(c, s, RING)))
                dve.wait_ge(u_made, state(b, c, s))
                for half in range(NH):
                    dve.wait_ge(a_made, state(b, c, s, NH) - (NH - 1 - half))
                    start = carry[:, half, s:s + 1] if c else 0.0
                    dve.tensor_tensor_scan(h[:, r, half], a_ps[:, half], u_in[:, r, half], start,
                                           ALU.mult, ALU.add).then_inc(h_done, 1)

            def split_rest(b, c):
                dve.wait_ge(hi_done, chunk(b, c + 1))
                dve.tensor_tensor(rest[:, :], scratch[0:2 * S, :], parts[:, 0, :], ALU.subtract).then_inc(emptied, 1)

            def split_lo(b, c):
                dve.wait_ge(mid_done, chunk(b, c + 1))
                dve.tensor_tensor(parts[:, 2, :], rest[:, :], parts[:, 1, :], ALU.subtract).then_inc(lo_done, 1)

            def softplus_sum(b, c):
                dve.wait_ge(ln_done, chunk(b, c + 1))
                dve.tensor_tensor(dt[:, (c + 1) % 2], xz[:, 0], xz[:, 1], ALU.add).then_inc(dt_done, 1)

            def dt_times_x(b, c):
                dve.wait_ge(dt_done, chunk(b, c + 1))
                dve.wait_ge(silu_done, chunk(b, c + 1))
                at = (c + 1) % 2
                dve.tensor_tensor(dtx[:, at], dt[:, at], xc[:, at], ALU.mult).then_inc(dtx_done, 1)

            def gate(b, c):
                dve.wait_ge(summed, state(b, c, S - 1))
                for half in range(NH):
                    dve.scalar_tensor_tensor(out=xc[:, c % 2, half], in0=xc[:, c % 2, half],
                                             scalar=d_skip[:, half:half + 1], in1=y_ps[:, half],
                                             op0=ALU.mult, op1=ALU.add).then_inc(skip_done, 1)
                dve.wait_ge(skip_done, chunk(b, c, NH))
                dve.tensor_tensor(xc[:, c % 2], xc[:, c % 2], zs[:, c % 2], ALU.mult).then_inc(gated, 1)

            def residual(b, c):
                dve.wait_ge(filled, used(b, "out", c))
                dve.wait_ge(base_done, chunk(b, c))
                dve.tensor_tensor(x2[:, c % 2], x2[:, c % 2], scratch[:, :], ALU.add).then_inc(emptied, 1)

            dve.wait_ge(raw_in, 3 * 16)
            for k in range(NC):
                last = raw_stats(k)
            last.then_inc(st, 1)
            dve.sem_inc(emptied, 1)
            group_local(0, "raw_first")
            group_deviation(0, "raw_first")
            group_shift(0, "raw_first")
            halo_scales(0)
            for k in range(BANDS):
                for step in range(len(DIL_SLOTS)):
                    dilate(0, k, step)
            dve.wait_ge(x1_in, C * 16)
            for k in range(NC):
                last = x1_stats(k)
            last.then_inc(st, 1)
            group_local(0, "x1_first")
            group_deviation(0, "x1_first")
            group_shift(0, "x1_first")
            normed(X1, g1[:, :], x1[:, 0:T]).then_inc(g1_done, 1)
            make_g1(0, -1)
            split_rest(0, -1)
            split_lo(0, -1)
            softplus_sum(0, -1)
            dt_times_x(0, -1)
            start_ahead(dve, u_made)
            start_ahead(dve, h_done, n=NH)
            with dve.Fori(0, B) as b:
                make_u(b, 0, 0)
                for c in range(NC):
                    for s in range(S):
                        if s + 1 < S or c + 1 < NC:
                            make_u(b, *behind(c, s, -1))
                        scan(b, c, s)
                        if s == OUT - 2 and c > 0:
                            gate(b, c - 1)
                        if s == OUT + 1 and c > 0:
                            residual(b, c - 1)
                        if s == XPROJ + 2:
                            split_rest(b, c)
                        if s == XPROJ + 4:
                            split_lo(b, c)
                        if s == DT_AT[-1] + 2:
                            softplus_sum(b, c)
                        if s == DT_AT[-1] + 3:
                            dt_times_x(b, c)
                        if c == RAW_STATS[0] and 0 <= s - RAW_STATS[1] < NC:
                            if s == RAW_STATS[1]:
                                dve.wait_ge(raw_in, (b + 2) * 3 * 16)
                            raw_stats(s - RAW_STATS[1])
                        if c == Z_STATS[0] and 0 <= s - Z_STATS[1] < NC:
                            if s == Z_STATS[1]:
                                dve.wait_ge(z_in, (b + 1) * BANDS * 16)
                            last = z_stats(Z0, s - Z_STATS[1])
                            if s - Z_STATS[1] == NC - 1:
                                last.then_inc(st, 1)
                                group_local(b, "joint")
                        if c == X1_STATS[0] and 0 <= s - X1_STATS[1] < NC:
                            if s == X1_STATS[1]:
                                dve.wait_ge(x1_in, (b + 2) * C * 16)
                            last = x1_stats(s - X1_STATS[1])
                            if s - X1_STATS[1] == NC - 1:
                                last.then_inc(st, 1)
                                group_local(b, "x1")
                        for name in MEAN_AT:
                            if MEAN_AT[name] == (c, s - 1):
                                group_deviation(b, name)
                            if VAR_AT[name] == (c, s - 2):
                                group_shift(b, name)
                                if name == "joint":
                                    halo_scales(b + 1)
                        for n in range(2):
                            if PADDED_AT[n] == (c, s):
                                pad(b, n)
                        if 1 <= c <= BANDS and s in DIL_SLOTS:
                            dilate(b + 1, c - 1, DIL_SLOTS.index(s))
                        for (n, k), (at_c, at_s) in CONV_AT.items():
                            if (at_c, at_s + 2) == (c, s):
                                add_conv(b, ("conv", n, k))
                                if (n, k) == (0, NC - 1):
                                    group_local(b, "z1")
                        if s == S - 1:
                            make_g1(b, c)
                gate(b, NC - 1)
                residual(b, NC - 1)
            dve.wait_ge(z_in, (B + 1) * BANDS * 16)
            for k in range(NC):
                last = z_stats(Z0, k)
            last.then_inc(st, 1)
            for n, name in enumerate(("z0_last", "z1_last")):
                group_local(B, name)
                group_deviation(B, name)
                group_shift(B, name)
                pad(B, n)
                for k in range(NC):
                    add_conv(B, ("conv_last", n, k))


def tables():
    import numpy as np

    group = np.kron(np.eye(4), np.full((32, 32), 1 / 32))
    in_comb = (np.arange(P) % (C * R)) // (2 * R)
    group_z = (in_comb[:, None] == in_comb[None, :]) / 32
    select = np.tile(np.kron(np.eye(S), np.ones((1, P))), (3, 1))
    band = np.arange(P) % NB
    top, bottom = (band > 0).astype(np.float64), (band < NB - 1).astype(np.float64)
    halo = np.stack([top, BORDER * (1 - top), bottom, BORDER * (1 - bottom)], axis=1)
    row = np.arange(P) // (C * R) * R + np.arange(P) % R
    taps = np.stack([row[:, None] == np.arange(BAND)[None, :] + kh - 1 for kh in range(3)], axis=1)
    said = {
        "center": np.eye(P) - 1 / P, "mean": np.full((P, P), 1 / P), "ident": np.eye(P), "group": group,
        "group_z": group_z, "halo": halo, "select": select, "taps": taps.reshape(P, 3 * BAND),
    }
    return {k: v.astype(np.float32) for k, v in said.items()}


def kernel(x, L1_conv_ln_gamma, L1_conv_ln_beta, L1_conv_in_proj_w, L1_conv_conv_w, L1_conv_conv_b,
           L1_conv_x_proj_w, L1_conv_dt_proj_w, L1_conv_dt_proj_b, L1_conv_A_log, L1_conv_D,
           L1_conv_out_proj_w, L2_conv_weight, L2_conv_bias, L3_conv_weight, L3_conv_bias):
    import numpy as np
    import concourse.bacc as bacc
    from concourse.bass_utils import run_bass_kernel_spmd

    def column(a):
        return np.asarray(a).reshape(-1, 1)

    xp = np.asarray(L1_conv_x_proj_w)
    scan_w = {
        "in_x_t": np.asarray(L1_conv_in_proj_w)[:DI].T, "in_z_t": np.asarray(L1_conv_in_proj_w)[DI:].T,
        "x_proj_t": np.concatenate([xp[DTR:], xp[:DTR]]).T,
        "out_proj_t": np.asarray(L1_conv_out_proj_w).T, "dt_proj_t": np.asarray(L1_conv_dt_proj_w).T,
        "conv_w_t": np.asarray(L1_conv_conv_w).reshape(DI, TAPS).T, "conv_b": column(L1_conv_conv_b),
        "dt_b": column(L1_conv_dt_proj_b), "d": column(L1_conv_D), "a_log": np.asarray(L1_conv_A_log),
        "gamma": column(L1_conv_ln_gamma), "beta": column(L1_conv_ln_beta),
    }
    convs = {}
    for n, (w, bias) in enumerate(((L2_conv_weight, L2_conv_bias), (L3_conv_weight, L3_conv_bias))):
        w = np.asarray(w)
        by_tap = w.transpose(1, 2, 3, 0).reshape(C, 9 * C)
        convs[f"main{n}"] = np.tile(np.repeat(by_tap, R, axis=0), (BANDS, 1))
        convs[f"above{n}"] = w[:, :, 0, :].transpose(2, 1, 0).reshape(3 * C, C)
        convs[f"below{n}"] = w[:, :, 2, :].transpose(2, 1, 0).reshape(3 * C, C)
        convs[f"bias{n}"] = np.tile(np.repeat(np.asarray(bias), R), BANDS).reshape(1, P)

    nc = bacc.Bacc("TRN2", target_bir_lowering=False, num_devices=1)
    arrays = {}

    def give(name, a):
        a = np.ascontiguousarray(a)
        arrays[name] = a
        return nc.dram_tensor(name, a.shape, mybir.dt.from_np(a.dtype), kind="ExternalInput").ap()

    x_in = give("x", x)
    scan_in = {k: give(f"mamba_{k}", v) for k, v in scan_w.items()}
    conv_in = {k: give(f"conv_{k}", v) for k, v in convs.items()}
    table_in = {k: give(f"table_{k}", v) for k, v in tables().items()}
    out = nc.dram_tensor("out", (B, C, H, W), F32, kind="ExternalOutput").ap()
    build(nc, x_in, scan_in, conv_in, table_in, out)
    return run_bass_kernel_spmd(nc, [arrays], core_ids=[0]).results[0]["out"]
```

```python
from contextlib import ExitStack

import concourse.bass as bass
from concourse import mybir

F32 = mybir.dt.float32
BF16 = mybir.dt.bfloat16
ALU = mybir.AluOpType
ACT = mybir.ActivationFunctionType

P = 128
B, C, H, W = 16, 8, 256, 256
R = 4
TH, TW = H // R, W // R
L = TH * TW
BAND = H // (P // C)
NB = H // BAND
BANDS = BAND // R
T = 512
NC = L // T
TROWS = T // TW
CB = T // W
DI = 256
NH = DI // P
S = 32
DTR = 8
TAPS = 4
PAD = TAPS - 1
XR = 2 * S + DTR
ER = 2 * 3 * C
BORDER = -2.0
EPS = 1e-5
RING = 2
C_RING = 4
LAG = 3
GS = 5
LOG_EXP = "natural_log_exp_and_others"

CENTER, VAR, OUT = 0, 1, 5
X_AT, Z_AT = ((4, 6, 7, 8), (9, 10, 11, 12)), ((13,), (14,))
XPROJ, DT_AT = (17, 18), ((20,), (22,))
SKIP, GATE, STORE_X2 = 2, 3, OUT + 1
SCALE, LAYER_NORM, BASE = VAR - 1, VAR + 2, 8
SILU, SPLIT_REST, SPLIT_MID, SPLIT_LO = 15, 18, 20, 20
SPLUS_IN, SOFTPLUS, SUM_DT, DT_X, NEXT_G1 = (21, 22), 23, (23, 25), (26, 28), 30
PLACES = ((15, 16, 19, 21), (23, 24, 25, 26), (28, 30, S + 2, S + 2))
CONV_AT = {}
for n, places in enumerate((((1, 0), (1, 1), (1, 2), (2, 0), (2, 1), (2, 2), (3, 0), (3, 1)),
                            ((4, 0), (4, 1), (4, 2), (5, 0), (5, 1), (5, 2), (6, 0), (7, 0)))):
    for k, (c, place) in enumerate(places):
        CONV_AT[n, k] = [c * S + s for s in PLACES[place]]
MEAN_AT = {"joint": (0, 23), "z1": (3, 29), "x1": (6, 24)}
VAR_AT = {"joint": (0, 26), "z1": (4, 0), "x1": (6, 26)}
DIL_SLOTS = (6, 8, 10, 12, 14, 16, 19)
PADDED_AT = ((0, 29), (4, 4))
LOAD_Z = (0, STORE_X2 + 1)
RAW_STATS, Z_STATS, X1_STATS = (0, 6), (0, 14), (6, 15)
X1_LOAD = (6, BASE + 1)

RAW, Z0, Z1, X1 = range(4)
NORMS = {"raw_first": (RAW, RAW + 1), "x1_first": (X1, X1 + 1), "joint": (RAW, Z0 + 1), "z1": (Z1, Z1 + 1),
         "x1": (X1, X1 + 1), "z0_last": (Z0, Z0 + 1), "z1_last": (Z1, Z1 + 1)}


def tensor_extras(c, s):
    at_state = {("center", c): [CENTER], ("var", c): [VAR], ("out", c): [OUT, OUT], ("xproj", c): XPROJ}
    for half in range(NH):
        at_state["x", c, half] = X_AT[half]
        at_state["z", c, half] = Z_AT[half]
        at_state["dt", c, half] = DT_AT[half]
    work = [(part, use) for use, states in at_state.items() for part, at in enumerate(states) if at == s]
    for (n, k), states in CONV_AT.items():
        work += [(part, ("conv", n, k)) for part, at in enumerate(states) if at == c * S + s]
    for name in MEAN_AT:
        if MEAN_AT[name] == (c, s):
            work.append((0, ("gn_mean", name)))
        if VAR_AT[name] == (c, s):
            work.append((0, ("gn_var", name)))
    return work


def n_parts(use):
    return {"x": TAPS, "conv": 4, "conv_last": 4, "out": NH, "out_last": NH, "xproj": NH}.get(use[0], 1)


def bank_of(use):
    return 0 if use[0] in ("center", "var", "x", "z", "xproj", "dt") else 1


FIRST_USES = [("gn_mean", "raw_first"), ("gn_var", "raw_first"), ("gn_mean", "x1_first"), ("gn_var", "x1_first"),
              ("center", -1), ("var", -1), ("x", -1, 0), ("x", -1, 1), ("z", -1, 0), ("z", -1, 1), ("xproj", -1),
              ("dt", -1, 0), ("dt", -1, 1)]
BODY_USES = [use for c in range(NC) for s in range(S) for part, use in tensor_extras(c, s)
             if part == n_parts(use) - 1]
LAST_USES = ([("out_last", 0), ("gn_mean", "z0_last"), ("gn_var", "z0_last")] + [("conv_last", 0, k) for k in range(NC)]
             + [("gn_mean", "z1_last"), ("gn_var", "z1_last")] + [("conv_last", 1, k) for k in range(NC)])
BY_BANK = [[[use for use in uses if bank_of(use) == bank] for uses in (FIRST_USES, BODY_USES, LAST_USES)]
           for bank in range(2)]


def build(nc, x, scan_w, conv_w, const, out):
    x1_dram = nc.dram_tensor("x1_dram", (C, TH, R, R, TW), F32, kind="Internal").ap()
    x2_dram = nc.dram_tensor("x2_dram", (TH, P, TW), F32, kind="Internal").ap()
    with ExitStack() as ctx:
        def sb(name, shape, dt=F32):
            return ctx.enter_context(nc.sbuf_tensor(name, shape, dt))

        def ps(name, shape):
            return ctx.enter_context(nc.psum_tensor(name, shape, F32))

        def sem(name):
            return ctx.enter_context(nc.semaphore(name))

        center_m = sb("center_m", [P, P])
        mean_m = sb("mean_m", [P, P])
        ident = sb("ident", [P, P])
        group_m = sb("group_m", [P, P])
        group_z = sb("group_z", [P, P])
        halo_keep = sb("halo_keep", [P, 4])
        select = sb("select", [3 * S, S * P], BF16)
        w_x = sb("w_x", [P, TAPS, DI])
        w_z = sb("w_z", [P, DI])
        w_xp = sb("w_xp", [P, NH, XR])
        w_dt = sb("w_dt", [2 * S + DTR, DI])
        w_out = sb("w_out", [P, NH, P])
        conv_bias = sb("conv_bias", [P, NH])
        dt_bias = sb("dt_bias", [P, NH])
        d_skip = sb("d_skip", [P, NH])
        a_neg = sb("a_neg", [P, NH * S])
        gamma = sb("gamma", [P, 1])
        beta = sb("beta", [P, 1])
        w_main = [sb(f"w_main{n}", [P, 3, P]) for n in range(2)]
        w_edge = [sb(f"w_edge{n}", [ER + 1, P]) for n in range(2)]
        eps_col = sb("eps_col", [P, 1])

        raw = sb("raw", [P, BAND + 2, W])
        norm = sb("norm", [P, R + 2, W + 2])
        vmax = sb("vmax", [P, R, W + 2])
        x1 = sb("x1", [P, L])
        z = sb("z", [P, L])
        padded = sb("padded", [P, NB + 2, W + 2])
        edge = sb("edge", [2 * S, 2, T])
        stats = sb("stats", [P, 4, NC, 6])
        mv = sb("mv", [P, 4, 2])
        g_mean = sb("g_mean", [P, 4])
        g_dev = sb("g_dev", [P, 4])
        g_var = sb("g_var", [P, 4])
        g_log = sb("g_log", [P, 4])
        g_rstd = sb("g_rstd", [P, 4])
        g_shift = sb("g_shift", [P, 4])
        halo = sb("halo", [P, 4])
        spare = sb("spare", [P, 1])

        g1 = sb("g1", [P, T])
        x2 = sb("x2", [P, 2, T])
        u_ln = sb("u_ln", [P, PAD + T])
        cen = sb("cen", [P, T])
        sq = sb("sq", [P, T])
        rstd = sb("rstd", [P, T])
        xz = sb("xz", [P, 2, NH, T])
        xc = sb("xc", [P, 2, NH, T])
        zs = sb("zs", [P, 2, NH, T])
        dt = sb("dt", [P, 2, NH, T])
        dtx = sb("dtx", [P, 2, NH, T])
        rest = sq[0:2 * S, :]
        parts = sb("parts", [2 * S, 3, T], BF16)
        dt_rows = cen
        b_parts = sb("b_parts", [3 * S, 2, T], BF16)
        c_parts = sb("c_parts", [3 * S, 2, T], BF16)
        u_in = sb("u_in", [P, RING, NH, T])
        h = sb("h", [P, RING, NH, T])
        hc = sb("hc", [P, RING, NH, T])
        a = sb("a", [P, RING, NH, T])
        c_sb = sb("c_sb", [P, C_RING, T])
        carry = sb("carry", [P, NH, S])

        proj_ps = ps("proj_ps", [P, T])
        side_ps = ps("side_ps", [P, T])
        b_ps = ps("b_ps", [P, 2, T])
        c_ps = ps("c_ps", [P, 2, T])
        y_ps = ps("y_ps", [P, NH, T])

        weights_in = sem("weights_in")
        edge_zero = sem("edge_weights_zero")
        select_in = sem("select_in")
        setup_v = sem("setup_v")
        setup_a = sem("setup_a")
        setup_p = sem("setup_p")
        proj_filled = sem("proj_ps_filled")
        proj_emptied = sem("proj_ps_emptied")
        side_filled = sem("side_ps_filled")
        side_emptied = sem("side_ps_emptied")
        raw_in = sem("raw_in")
        dil = sem("dilation_steps")
        x1_rows_out = sem("x1_rows_out")
        x1_in = sem("x1_patch_in")
        st = sem("group_stats")
        gs = sem("group_norm_steps")
        ga = sem("group_rstd")
        g1_done = sem("g1_done")
        base_done = sem("x1_plus_g1")
        x2_out = sem("x2_chunk_out")
        z_in = sem("z_in")
        padded_done = sem("padded_done")
        edge_in = [sem(f"edge_rows_in{k}") for k in range(2)]
        stored = sem("stored")
        carry_u = sem("u_tail_kept")
        rstd_done = sem("rstd_done")
        scaled = sem("token_scaled")
        u_done = sem("u_ln_done")
        silu_done = sem("silu_done")
        hi_done = sem("part_hi")
        mid_done = sem("part_mid")
        lo_done = sem("part_lo")
        parts_in = sem("parts_moved")
        exp_done = sem("dt_exp")
        ln_done = sem("dt_ln")
        dt_done = sem("dt_done")
        dtx_done = sem("dtx_done")
        b_cast = sem("b_broadcast")
        c_cast = sem("c_broadcast")
        u_made = sem("state_input")
        a_made = sem("decay")
        c_copied = sem("c_copied")
        h_done = sem("h_done")
        kept = sem("carry_kept")
        hc_done = sem("hc_done")
        summed = sem("y_summed")
        skip_done = sem("y_plus_skip")
        gated = sem("y_gated")

        block = ctx.enter_context(nc.Block())

        def used(b, *use):
            first, body, last = BY_BANK[bank_of(use)]
            if use in first:
                return first.index(use) + 1
            if use in last:
                return len(first) + B * len(body) + last.index(use) + 1
            return b * len(body) + len(first) + body.index(use) + 1

        def read(b, *use):
            return used(b, *use) + 1

        def norm_number(b, name):
            if name in ("raw_first", "x1_first"):
                return ("raw_first", "x1_first").index(name)
            if name in ("z0_last", "z1_last"):
                return 2 + 3 * B + ("z0_last", "z1_last").index(name)
            return b * 3 + 2 + ("joint", "z1", "x1").index(name)

        def chunk(b, c, n=1):
            return (b * NC + (c + 1)) * n

        def state(b, c, s, n=1):
            return (b * (NC * S) + (c * S + s + 1 + C_RING)) * n

        def start_ahead(engine, *semaphores, n=1):
            for semaphore in semaphores:
                engine.sem_inc(semaphore, C_RING * n)

        def kept_state(b, c, s):
            return b * ((NC - 1) * S) + (c * S + s + 1)

        def behind(c, s, n):
            at = c * S + s - n
            return at // S, at % S

        N_WEIGHTS = 33
        SETUP_V = 4 + TAPS + 2 * (9 + 6)
        SETUP_P = 8
        DIL_AT = [4 + 6 * (k + 1) + 1 + (k == BANDS - 1) for k in range(BANDS)]
        DIL = DIL_AT[-1]

        @block.sync
        def _(sp):
            def load(dst, src):
                sp.dma_start(dst, src).then_inc(weights_in, 16)

            load(center_m[:, :], const["center"])
            load(mean_m[:, :], const["mean"])
            load(ident[:, :], const["ident"])
            load(group_m[:, :], const["group"])
            load(group_z[:, :], const["group_z"])
            load(halo_keep[:, :], const["halo"])
            load(w_x[:, 0, :], scan_w["in_x_t"])
            load(w_z[:, :], scan_w["in_z_t"])
            for half in range(NH):
                rows = slice(half * P, (half + 1) * P)
                load(w_xp[:, half, :], scan_w["x_proj_t"][rows, :])
                load(w_out[:, half, :], scan_w["out_proj_t"][rows, :])
                load(conv_bias[:, half:half + 1], scan_w["conv_b"][rows, :])
                load(dt_bias[:, half:half + 1], scan_w["dt_b"][rows, :])
                load(d_skip[:, half:half + 1], scan_w["d"][rows, :])
                load(a_neg[:, half * S:(half + 1) * S], scan_w["a_log"][rows, :])
            load(w_dt[2 * S:, :], scan_w["dt_proj_t"])
            load(gamma[:, :], scan_w["gamma"])
            load(beta[:, :], scan_w["beta"])
            load(norm[:, 0:TAPS, 0:DI], scan_w["conv_w_t"].partition_broadcast(P))
            load(sq[:, 144:192], const["taps"])
            for n in range(2):
                load(sq[:, 72 * n:72 * (n + 1)], conv_w[f"main{n}"])
            sp.wait_ge(edge_zero, 2)
            for n in range(2):
                with nc.allow_non_contiguous_dma(reason="a few weights, once"):
                    load(w_edge[n][0:ER // 2, 0:C * R:R], conv_w[f"above{n}"])
                    load(w_edge[n][ER // 2:ER, P - C * R + R - 1:P:R], conv_w[f"below{n}"])
                load(w_edge[n][ER:ER + 1, :], conv_w[f"bias{n}"])
            sp.dma_start(x1[0:3 * S, :], const["select"]).then_inc(select_in, 16)

            def load_raw(image):
                img = x[bass.ds(image, 1)].rearrange("o c (g r) w -> (o c g) (r w)", r=BAND)
                sp.dma_start(raw[:, 1:BAND + 1, :], img).then_inc(raw_in, 16)
                sp.dma_start(raw[1:P, 0:1, :], img[0:P - 1, (BAND - 1) * W:]).then_inc(raw_in, 16)
                sp.dma_start(raw[0:P - 1, BAND + 1:, :], img[1:P, 0:W]).then_inc(raw_in, 16)

            def store_x1_rows(number, k):
                sp.wait_ge(dil, number * DIL + DIL_AT[k])
                sp.dma_start(x1_dram.rearrange("c (g l) r q w -> l (c g) r (q w)", l=BANDS)[k],
                             vmax[:, :, 0:W]).then_inc(x1_rows_out, 16)

            def load_x1(number):
                sp.wait_ge(x1_rows_out, number * (BANDS * 16) + BANDS * 16)
                for ch in range(C):
                    sp.dma_start(x1[ch * R * R:(ch + 1) * R * R, :].rearrange("p (t w) -> p t w", w=TW),
                                 x1_dram[ch].rearrange("t r q w -> (r q) t w")).then_inc(x1_in, 16)

            def move_parts(b, c):
                sp.wait_ge(lo_done, chunk(b, c + 1))
                for k in range(3):
                    for rows, to in ((slice(0, S), b_parts), (slice(S, 2 * S), c_parts)):
                        sp.dma_start(to[k * S:(k + 1) * S, (c + 1) % 2, :], parts[rows, k, :]).then_inc(parts_in, 16)

            def store_x2(b, use):
                c = use[1]
                sp.wait_ge(side_emptied, read(b, *use))
                if c == 1:
                    sp.wait_ge(z_in, b * (BANDS * 16) + BANDS * 16)
                at = (c - 1) % NC
                sp.dma_start(x2_dram[at * TROWS:(at + 1) * TROWS].rearrange("t p w -> p t w"),
                             x2[:, (c + 1) % 2].rearrange("p (t w) -> p t w", w=TW)).then_inc(x2_out, 16)

            def load_z(b):
                sp.wait_ge(x2_out, chunk(b, 0, 16) + 16)
                for k in range(BANDS):
                    sp.dma_start(z[k * C * R:(k + 1) * C * R, :].rearrange("p (g w) -> p g w", g=NB),
                                 z_source(k)).then_inc(z_in, 16)

            def z_source(k):
                return x2_dram.rearrange("t p w -> t (p w)").rearrange("(g l) (m v) -> l m g v", l=BANDS, v=W)[k]

            def load_edge(b, n, k, conv="conv"):
                if k < 2:
                    sp.wait_ge(padded_done, b * 2 + n + 1)
                else:
                    sp.wait_ge(side_filled, used(b, conv, n, k - 2))
                for dw in range(3):
                    sp.dma_start(edge[dw * C:(dw + 1) * C, k % 2, :].rearrange("p (g w) -> p g w", w=W),
                                 padded[P - C * R + R - 1:P:R, CB * k:CB * (k + 1), dw:dw + W]).then_inc(edge_in[k % 2], 16)
                    sp.dma_start(edge[(3 + dw) * C:(4 + dw) * C, k % 2, :].rearrange("p (g w) -> p g w", w=W),
                                 padded[0:C * R:R, CB * k + 2:CB * (k + 1) + 2, dw:dw + W]).then_inc(edge_in[k % 2], 16)

            def store_output(b, image, conv="conv"):
                sp.wait_ge(side_emptied, read(b, conv, 1, NC - 1))
                for k in range(BANDS):
                    for r in range(R):
                        rows = raw[k * C * R + r:(k + 1) * C * R:R, 1:BAND + 1, :]
                        sp.dma_start(out_rows(image, k * R + r), rows).then_inc(stored, 16)

            def out_rows(image, r):
                return out[bass.ds(image, 1)].rearrange("o c (g r) w -> r (o c) g w", r=BAND)[r]

            sp.wait_ge(setup_p, SETUP_P)
            sp.wait_ge(setup_v, SETUP_V)
            sp.dma_start(x2_dram.rearrange("t p w -> p t w"),
                         z[:, :].rearrange("p (t w) -> p t w", w=TW)).then_inc(x2_out, 16)
            load_raw(0)
            for k in range(BANDS):
                store_x1_rows(0, k)
            sp.wait_ge(setup_a, 2)
            load_x1(0)
            move_parts(0, -1)
            sp.sem_inc(stored, BAND * 16)
            with sp.Fori(0, B) as b:
                image_ahead, image_behind = sp.snap((b + 1) % B), sp.snap((b + (B - 1)) % B)
                for c in range(NC):
                    for s in range(S):
                        if (c, s) == (0, 0):
                            sp.wait_ge(stored, b * (BAND * 16) + BAND * 16)
                            load_raw(image_ahead)
                        if s == STORE_X2:
                            store_x2(b, ("out", c))
                        if (c, s) == LOAD_Z:
                            load_z(b)
                        if s == SPLIT_LO:
                            move_parts(b, c)
                        if s == DIL_SLOTS[-1] and 1 <= c <= BANDS:
                            store_x1_rows(b + 1, c - 1)
                        if (c, s) == X1_LOAD:
                            sp.wait_ge(base_done, chunk(b, NC - 1))
                            load_x1(b + 1)
                        for n in range(2):
                            if (c, s) == PADDED_AT[n]:
                                load_edge(b, n, 0)
                                load_edge(b, n, 1)
                            for k in range(2, NC):
                                if CONV_AT[n, k - 2][-1] == c * S + s:
                                    load_edge(b, n, k)
                        if CONV_AT[1, NC - 1][-1] + 2 == c * S + s:
                            store_output(b, image_behind)
            sp.wait_ge(stored, (B + 1) * BAND * 16)
            store_x2(B, ("out_last", 0))
            load_z(B)
            for n in range(2):
                for k in range(NC):
                    load_edge(B, n, k, "conv_last")
            store_output(B, B - 1, "conv_last")
            sp.wait_ge(stored, (B + 2) * BAND * 16)

        @block.gpsimd
        def _(pool):
            pool.memset(w_edge[0][:, :], 0.0).then_inc(edge_zero, 1)
            pool.memset(w_edge[1][:, :], 0.0).then_inc(edge_zero, 1)
            pool.memset(raw[:, :, :], 0.0).then_inc(setup_p, 1)
            pool.memset(padded[:, :, :], 0.0).then_inc(setup_p, 1)
            pool.memset(edge[:, :, :], 1.0).then_inc(setup_p, 1)
            pool.memset(z[:, :], 0.0).then_inc(setup_p, 1)
            for nothing in (xc[:, 1], zs[:, 1], x2[:, 1, :], hc[:, :, :, :]):
                pool.memset(nothing, 0.0).then_inc(setup_p, 1)

            def scale_tokens(b, c):
                pool.wait_ge(rstd_done, chunk(b, c + 1))
                pool.tensor_tensor(cen[:, :], cen[:, :], rstd[:, :], ALU.mult).then_inc(scaled, 1)

            def make_base(b, c):
                pool.wait_ge(g1_done, chunk(b, c + 1))
                pool.wait_ge(x2_out, chunk(b, c, 16) + 16)
                at = (c + 1) % NC
                pool.tensor_tensor(x2[:, at % 2], x1[:, at * T:(at + 1) * T], g1[:, :], ALU.add).then_inc(base_done, 1)

            def softplus_sum(b, c, half):
                pool.wait_ge(ln_done, chunk(b, c + 1))
                pool.tensor_tensor(dt[:, (c + 1) % 2, half], xz[:, 0, half], xz[:, 1, half],
                                   ALU.add).then_inc(dt_done, 1)

            def dt_times_x(b, c, half):
                pool.wait_ge(dt_done, chunk(b, c + 1, NH) - (NH - 1 - half))
                pool.wait_ge(silu_done, chunk(b, c + 1))
                at = (c + 1) % 2
                pool.tensor_tensor(dtx[:, at, half], dt[:, at, half], xc[:, at, half], ALU.mult).then_inc(dtx_done, 1)

            pool.wait_ge(g1_done, 1)
            pool.tensor_tensor(x2[:, 0], x1[:, 0:T], g1[:, :], ALU.add).then_inc(base_done, 1)
            scale_tokens(0, -1)
            for half in range(NH):
                softplus_sum(0, -1, half)
            for half in range(NH):
                dt_times_x(0, -1, half)
            start_ahead(pool, hc_done)
            with pool.Fori(0, B) as b:
                for c in range(NC):
                    for s in range(S):
                        pool.wait_ge(c_copied, state(b, c, s))
                        pool.wait_ge(h_done, state(b, c, s, NH))
                        pool.wait_ge(summed, state(b, *behind(c, s, RING)))
                        pool.tensor_tensor(hc[:, s % RING], h[:, s % RING],
                                           c_sb[:, s % C_RING:s % C_RING + 1, :].broadcast_to([P, NH, T]), ALU.mult).then_inc(hc_done, 1)
                        if s == SCALE:
                            scale_tokens(b, c)
                        if s == BASE:
                            make_base(b, c)
                        for half in range(NH):
                            if s == SUM_DT[half]:
                                softplus_sum(b, c, half)
                            if s == DT_X[half]:
                                dt_times_x(b, c, half)

        @block.scalar
        def _(act):
            act.preload_act_table_set(LOG_EXP)
            act.wait_ge(weights_in, N_WEIGHTS * 16)
            act.activation(a_neg[:, :], a_neg[:, :], ACT.Exp).then_inc(setup_a, 1)
            act.wait_ge(select_in, 16)
            act.activation(select[:, :], x1[0:3 * S, :], ACT.Copy).then_inc(setup_a, 1)
            act.wait_ge(setup_v, 1)

            def group_rstd(b, name):
                lo, hi = NORMS[name]
                act.wait_ge(side_filled, used(b, "gn_var", name))
                act.activation(g_log[:, lo:hi], side_ps[:, 0:hi - lo], ACT.Ln, bias=eps_col[:, :]).then_inc(side_emptied, 1)
                act.wait_ge(side_emptied, read(b, "gn_var", name))
                act.activation(g_rstd[:, lo:hi], g_log[:, lo:hi], ACT.Exp, scale=-0.5).then_inc(ga, 1)

            def centered(b, c):
                act.wait_ge(proj_filled, used(b, "center", c))
                act.activation(cen[:, :], proj_ps[:, :], ACT.Copy)
                act.activation(sq[:, :], proj_ps[:, :], ACT.Square).then_inc(proj_emptied, 1)

            def token_rstd(b, c):
                act.wait_ge(proj_filled, used(b, "var", c))
                act.activation(rstd[:, :], proj_ps[:, :], ACT.Ln, bias=eps_col[:, :]).then_inc(proj_emptied, 1)
                act.wait_ge(proj_emptied, read(b, "var", c))
                act.activation(rstd[:, :], rstd[:, :], ACT.Exp, scale=-0.5).then_inc(rstd_done, 1)

            def layer_norm(b, c):
                if (c + 1) % NC:
                    act.activation(u_ln[:, 0:PAD], u_ln[:, T:T + PAD], ACT.Copy).then_inc(carry_u, 1)
                else:
                    act.memzero(u_ln[:, 0:PAD]).then_inc(carry_u, 1)
                act.wait_ge(carry_u, chunk(b, c + 1))
                act.wait_ge(scaled, chunk(b, c + 1))
                act.activation(u_ln[:, PAD:], cen[:, :], ACT.Identity, bias=beta[:, :],
                               scale=gamma[:, :]).then_inc(u_done, 1)

            def copy_x(b, c, half):
                act.wait_ge(proj_filled, used(b, "x", c, half))
                act.activation(xz[:, 0, half], proj_ps[:, :], ACT.Identity,
                               bias=conv_bias[:, half:half + 1]).then_inc(proj_emptied, 1)

            def copy_z(b, c, half):
                act.wait_ge(proj_filled, used(b, "z", c, half))
                act.activation(xz[:, 1, half], proj_ps[:, :], ACT.Copy).then_inc(proj_emptied, 1)

            def silus(b, c):
                act.wait_ge(proj_emptied, read(b, "z", c, NH - 1))
                act.activation(xc[:, (c + 1) % 2], xz[:, 0], ACT.Silu)
                act.activation(zs[:, (c + 1) % 2], xz[:, 1], ACT.Silu).then_inc(silu_done, 1)
                act.preload_act_table_set(LOG_EXP)

            def split_hi(b, c):
                act.wait_ge(proj_filled, used(b, "xproj", c))
                act.activation(dt_rows[2 * S:XR, :], proj_ps[2 * S:XR, :], ACT.Copy)
                act.activation(parts[:, 0, :], proj_ps[0:2 * S, :], ACT.Copy).then_inc(hi_done, 1)

            def split_mid(b, c):
                act.wait_ge(proj_emptied, read(b, "xproj", c))
                act.activation(parts[:, 1, :], rest[:, :], ACT.Copy).then_inc(mid_done, 1)

            def softplus_in(b, c, half):
                act.wait_ge(proj_filled, used(b, "dt", c, half))
                act.activation(xz[:, 0, half], proj_ps[:, :], ACT.Abs, bias=dt_bias[:, half:half + 1])
                act.activation(xz[:, 1, half], proj_ps[:, :], ACT.Relu,
                               bias=dt_bias[:, half:half + 1]).then_inc(proj_emptied, 1)

            def softplus_log(b, c):
                act.wait_ge(proj_emptied, read(b, "dt", c, NH - 1))
                act.activation(xz[:, 0], xz[:, 0], ACT.Exp, scale=-1.0).then_inc(exp_done, 1)
                act.wait_ge(exp_done, chunk(b, c + 1))
                act.activation(xz[:, 0], xz[:, 0], ACT.Ln, bias=1.0).then_inc(ln_done, 1)

            def make_decay(b, c, s):
                if s == 0:
                    act.wait_ge(dt_done, chunk(b, c, NH))
                for half in range(NH):
                    act.wait_ge(h_done, state(b, *behind(c, s, RING), NH) - (NH - 1 - half))
                    at = half * S + s
                    act.activation(a[:, s % RING, half], dt[:, c % 2, half], ACT.Exp,
                                   scale=a_neg[:, at:at + 1]).then_inc(a_made, 1)

            def keep(b, c, s):
                act.wait_ge(h_done, state(b, c, s, NH))
                act.activation(carry[:, :, s:s + 1], h[:, s % RING, :, T - 1:T], ACT.Copy).then_inc(kept, 1)

            group_rstd(0, "raw_first")
            group_rstd(0, "x1_first")
            centered(0, -1)
            token_rstd(0, -1)
            layer_norm(0, -1)
            for half in range(NH):
                copy_x(0, -1, half)
            for half in range(NH):
                copy_z(0, -1, half)
            silus(0, -1)
            split_hi(0, -1)
            split_mid(0, -1)
            softplus_in(0, -1, 0)
            softplus_in(0, -1, 1)
            softplus_log(0, -1)
            start_ahead(act, c_copied)
            start_ahead(act, a_made, n=NH)
            with act.Fori(0, B) as b:
                make_decay(b, 0, 0)
                for c in range(NC):
                    for s in range(S):
                        if s + 1 < S or c + 1 < NC:
                            make_decay(b, *behind(c, s, -1))
                        act.wait_ge(c_cast, state(b, c, s))
                        act.wait_ge(hc_done, state(b, *behind(c, s, C_RING)))
                        act.activation(c_sb[:, s % C_RING], c_ps[:, s % 2], ACT.Copy).then_inc(c_copied, 1)
                        if (c or s) and (c < NC - 1 or s == 0):
                            keep(b, *behind(c, s, 1))
                        if s == CENTER:
                            centered(b, c)
                        if s == VAR:
                            token_rstd(b, c)
                        if s == LAYER_NORM:
                            layer_norm(b, c)
                        for half in range(NH):
                            if s == X_AT[half][-1]:
                                copy_x(b, c, half)
                            if s == Z_AT[half][-1]:
                                copy_z(b, c, half)
                            if s == SPLUS_IN[half]:
                                softplus_in(b, c, half)
                        if s == SILU:
                            silus(b, c)
                        if s == XPROJ[-1]:
                            split_hi(b, c)
                        if s == SPLIT_MID:
                            split_mid(b, c)
                        if s == SOFTPLUS:
                            softplus_log(b, c)
                        for name in VAR_AT:
                            if VAR_AT[name] == (c, s - 1):
                                group_rstd(b, name)
            group_rstd(B, "z0_last")
            group_rstd(B, "z1_last")

        @block.tensor
        def _(pe):
            pe.wait_ge(weights_in, N_WEIGHTS * 16)
            pe.wait_ge(setup_v, SETUP_V)
            pe.wait_ge(setup_a, 2)
            pe.wait_ge(setup_p, SETUP_P)

            def take_scratch(b, *use):
                pe.wait_ge(proj_emptied if bank_of(use) == 0 else side_emptied, used(b, *use))

            def group_product(b, name, rhs):
                lo, hi = NORMS[name]
                for n in range(lo, hi):
                    mm = pe.matmul(side_ps[:, n - lo:n - lo + 1], (group_z if n in (Z0, Z1) else group_m)[:, :],
                                   rhs(n), start=True, stop=True, skip_group_check=True)
                mm.then_inc(side_filled, 1)

            def group_mean(b, name):
                pe.wait_ge(gs, norm_number(b, name) * GS + 1)
                take_scratch(b, "gn_mean", name)
                group_product(b, name, lambda n: mv[:, n, 0:1])

            def group_var(b, name):
                pe.wait_ge(gs, norm_number(b, name) * GS + 4)
                take_scratch(b, "gn_var", name)
                group_product(b, name, lambda n: g_var[:, n:n + 1])

            def center(b, c):
                pe.wait_ge(g1_done, chunk(b, c + 1))
                take_scratch(b, "center", c)
                pe.matmul(proj_ps[:, :], center_m[:, :], g1[:, :], start=True, stop=True).then_inc(proj_filled, 1)

            def variance(b, c):
                take_scratch(b, "var", c)
                pe.matmul(proj_ps[:, :], mean_m[:, :], sq[:, :], start=True, stop=True).then_inc(proj_filled, 1)

            def project_x(b, c, half, tap):
                if tap == 0:
                    pe.wait_ge(u_done, chunk(b, c + 1))
                    take_scratch(b, "x", c, half)
                mm = pe.matmul(proj_ps[:, :], w_x[:, tap, half * P:(half + 1) * P], u_ln[:, tap:tap + T],
                               start=(tap == 0), stop=(tap == TAPS - 1), skip_group_check=True)
                if tap == TAPS - 1:
                    mm.then_inc(proj_filled, 1)

            def project_z(b, c, half):
                take_scratch(b, "z", c, half)
                pe.matmul(proj_ps[:, :], w_z[:, half * P:(half + 1) * P], u_ln[:, PAD:],
                          start=True, stop=True).then_inc(proj_filled, 1)

            def x_proj(b, c, half):
                if half == 0:
                    pe.wait_ge(silu_done, chunk(b, c + 1))
                    take_scratch(b, "xproj", c)
                mm = pe.matmul(proj_ps[0:XR, :], w_xp[:, half, :], xc[:, (c + 1) % 2, half],
                               start=(half == 0), stop=(half == NH - 1), skip_group_check=True)
                if half == NH - 1:
                    mm.then_inc(proj_filled, 1)

            def dt_proj(b, c, half):
                pe.wait_ge(hi_done, chunk(b, c + 1))
                take_scratch(b, "dt", c, half)
                pe.matmul(proj_ps[:, :], w_dt[2 * S:XR, half * P:(half + 1) * P], dt_rows[2 * S:XR, :],
                          start=True, stop=True).then_inc(proj_filled, 1)

            def out_proj(b, use, half):
                c = use[1]
                if half == 0:
                    pe.wait_ge(gated, chunk(b, c))
                    take_scratch(b, *use)
                mm = pe.matmul(side_ps[:, :], w_out[:, half, :], xc[:, (c + 1) % 2, half],
                               start=(half == 0), stop=(half == NH - 1), skip_group_check=True)
                if half == NH - 1:
                    mm.then_inc(side_filled, 1)

            def sum_states(b, c, s):
                pe.wait_ge(hc_done, state(b, c, s))
                for half in range(NH):
                    if s == 0:
                        pe.wait_ge(skip_done, chunk(b, c, NH) - (NH - 1 - half))
                    mm = pe.matmul(y_ps[:, half], ident[:, :], hc[:, s % RING, half],
                                   start=(s == 0), stop=(s == S - 1), skip_group_check=True)
                mm.then_inc(summed, 1)

            def convolve(b, use, part):
                _, n, k = use
                if part == 0:
                    pe.wait_ge(padded_done, b * 2 + n + 1)
                    take_scratch(b, *use)
                if part < 3:
                    pe.matmul(side_ps[:, :].rearrange("p (g w) -> p g w", w=W), w_main[n][:, part, :],
                              padded[:, 1 + CB * k:1 + CB * (k + 1), part:part + W],
                              start=(part == 0), stop=False, skip_group_check=True)
                else:
                    pe.wait_ge(edge_in[k % 2], b * (NC * 6 * 16) + ((n * NC + k) // 2 + 1) * (6 * 16))
                    pe.matmul(side_ps[:, :], w_edge[n][:, :], edge[0:ER + 1, k % 2, :],
                              start=False, stop=True, skip_group_check=True).then_inc(side_filled, 1)

            def extra(b, part, use):
                name, *at = use
                if name in ("conv", "conv_last"):
                    convolve(b, use, part)
                elif name in ("out", "out_last"):
                    out_proj(b, use, part)
                elif name == "x":
                    project_x(b, *at, part)
                elif name == "xproj":
                    x_proj(b, *at, part)
                else:
                    {"center": center, "var": variance, "z": project_z, "dt": dt_proj,
                     "gn_mean": group_mean, "gn_var": group_var}[name](b, *at)

            for half in range(NH):
                mm = pe.matmul(y_ps[:, half], ident[:, :], hc[:, 0, half], start=True, stop=False,
                               skip_group_check=True)
            for use in FIRST_USES:
                for part in range(n_parts(use)):
                    extra(0, part, use)
            start_ahead(pe, b_cast, c_cast)
            pe.sem_inc(summed, C_RING - LAG)
            with pe.Fori(0, B) as b:
                for c in range(NC):
                    pe.wait_ge(parts_in, chunk(b, c, 6 * 16))
                    for s in range(S):
                        sel = select[:, s * P:(s + 1) * P]
                        pe.wait_ge(u_made, state(b, *behind(c, s, 2)))
                        pe.matmul(b_ps[:, s % 2], sel, b_parts[:, c % 2, :], start=True, stop=True).then_inc(b_cast, 1)
                        pe.wait_ge(c_copied, state(b, *behind(c, s, 2)))
                        pe.matmul(c_ps[:, s % 2], sel, c_parts[:, c % 2, :], start=True, stop=True).then_inc(c_cast, 1)
                        sum_states(b, *behind(c, s, LAG))
                        for part, use in tensor_extras(c, s):
                            extra(b, part, use)
            for s in range(LAG):
                sum_states(B, *behind(0, s, LAG))
            for use in LAST_USES:
                for part in range(n_parts(use)):
                    extra(B, part, use)

        @block.vector
        def _(dve):
            steps = 0

            def own(ins):
                nonlocal steps
                steps += 1
                ins.then_inc(setup_v, 1)
                dve.wait_ge(setup_v, steps)

            own(dve.memset(eps_col[:, :], EPS))
            dve.wait_ge(weights_in, N_WEIGHTS * 16)
            dve.wait_ge(setup_a, 1)
            own(dve.tensor_scalar(a_neg[:, :], a_neg[:, :], -1.0, None, ALU.mult))
            for k in reversed(range(TAPS)):
                own(dve.tensor_tensor(w_x[:, k, :], w_x[:, 0, :], norm[:, k, 0:DI], ALU.mult))
            own(dve.memset(norm[:, :, :], BORDER))
            own(dve.memset(spare[:, :], 0.0))
            for n in range(2):
                for dw in range(3):
                    for kh in range(3):
                        j = 72 * n + C * (3 * kh + dw)
                        w = sq[:, j:j + C].unsqueeze(1).unsqueeze(3)
                        at = sq[:, 144 + 16 * kh:144 + 16 * (kh + 1)].rearrange("p (l r) -> p l r", r=R).unsqueeze(2)
                        dst = cen[:, 0:P] if kh else w_main[n][:, dw, :]
                        own(dve.tensor_tensor(dst.rearrange("p (l c r) -> p l c r", l=BANDS, c=C),
                                              w.broadcast_to([P, BANDS, C, R]), at.broadcast_to([P, BANDS, C, R]),
                                              ALU.mult))
                        if kh:
                            own(dve.tensor_tensor(w_main[n][:, dw, :], w_main[n][:, dw, :], cen[:, 0:P], ALU.add))

            def partition_stats(kind, k, src):
                return dve.bn_stats(stats[:, kind, k, :], src)

            def raw_stats(k):
                return partition_stats(RAW, k, raw[:, 1 + 2 * k:3 + 2 * k, :].rearrange("p a w -> p (a w)"))

            def z_stats(kind, k):
                return partition_stats(kind, k, z[:, k * T:(k + 1) * T])

            def x1_stats(k):
                return partition_stats(X1, k, x1[:, k * T:(k + 1) * T])

            def group_local(b, name):
                lo, hi = NORMS[name]
                dve.wait_ge(st, norm_number(b, name) + 1)
                dve.memset(spare[:, :], 0.0)
                for n in range(lo, hi):
                    last = dve.bn_aggr(mv[:, n, :], stats[:, n, :, :])
                last.then_inc(gs, 1)

            def group_deviation(b, name):
                lo, hi = NORMS[name]
                at = norm_number(b, name) * GS
                dve.wait_ge(side_filled, used(b, "gn_mean", name))
                dve.tensor_copy(g_mean[:, lo:hi], side_ps[:, 0:hi - lo]).then_inc(side_emptied, 1)
                dve.wait_ge(side_emptied, read(b, "gn_mean", name))
                dve.tensor_tensor(g_dev[:, lo:hi], mv[:, lo:hi, 0], g_mean[:, lo:hi], ALU.subtract).then_inc(gs, 1)
                dve.wait_ge(gs, at + 2)
                dve.tensor_tensor(g_dev[:, lo:hi], g_dev[:, lo:hi], g_dev[:, lo:hi], ALU.mult).then_inc(gs, 1)
                dve.wait_ge(gs, at + 3)
                dve.tensor_tensor(g_var[:, lo:hi], g_dev[:, lo:hi], mv[:, lo:hi, 1], ALU.add).then_inc(gs, 1)

            def group_shift(b, name):
                lo, hi = NORMS[name]
                dve.wait_ge(ga, norm_number(b, name) + 1)
                dve.scalar_tensor_tensor(out=g_shift[:, lo:hi], in0=g_mean[:, lo:hi], scalar=-1.0,
                                         in1=g_rstd[:, lo:hi], op0=ALU.mult, op1=ALU.mult).then_inc(gs, 1)
                dve.wait_ge(gs, norm_number(b, name) * GS + 5)

            def normed(kind, dst, src):
                return dve.tensor_scalar(dst, src, g_rstd[:, kind:kind + 1], g_shift[:, kind:kind + 1],
                                         ALU.mult, ALU.add)

            def scale_step(number, at, ins):
                ins.then_inc(dil, 1)
                dve.wait_ge(dil, number * DIL + at)

            def halo_scales(number):
                for side in range(2):
                    keep, fill = halo_keep[:, 2 * side:2 * side + 1], halo_keep[:, 2 * side + 1:2 * side + 2]
                    scale_step(number, 1 + 2 * side,
                               dve.tensor_scalar(halo[:, 2 * side:2 * side + 1], keep, g_rstd[:, RAW:RAW + 1], None,
                                                    ALU.mult))
                    scale_step(number, 2 + 2 * side,
                               dve.scalar_tensor_tensor(out=halo[:, 2 * side + 1:2 * side + 2], in0=keep,
                                                           scalar=g_shift[:, RAW:RAW + 1], in1=fill,
                                                           op0=ALU.mult, op1=ALU.add))

            def dilate(number, k, step):
                at = 4 + 6 * k + (k > 0) + step + 1
                inner = slice(1, W + 1)
                top = norm[:, 1:R + 1, inner]
                has_halo = k in (0, BANDS - 1)
                if step < 6 + has_halo:
                    dve.wait_ge(dil, number * DIL + at - 1)
                if step == 0:
                    first, last = (1 if k == 0 else 0), (R + 1 if k == BANDS - 1 else R + 2)
                    ins = normed(RAW, norm[:, first:last, inner], raw[:, k * R + first:k * R + last, :])
                elif has_halo and step == 1:
                    side, row = (0, 0) if k == 0 else (1, R + 1)
                    ins = dve.tensor_scalar(norm[:, row:row + 1, inner], raw[:, k * R + row:k * R + row + 1, :],
                                            halo[:, 2 * side:2 * side + 1], halo[:, 2 * side + 1:2 * side + 2],
                                            ALU.mult, ALU.add)
                elif step == 1 + has_halo:
                    if k:
                        dve.wait_ge(x1_rows_out, number * (BANDS * 16) + k * 16)
                    ins = dve.tensor_tensor(vmax[:, :, :], norm[:, 0:R, :], norm[:, 1:R + 1, :], ALU.max)
                elif step == 2 + has_halo:
                    ins = dve.tensor_tensor(vmax[:, :, :], vmax[:, :, :], norm[:, 2:R + 2, :], ALU.max)
                elif step == 3 + has_halo:
                    ins = dve.tensor_tensor(top, vmax[:, :, 0:W], vmax[:, :, 1:W + 1], ALU.max)
                elif step == 4 + has_halo:
                    ins = dve.tensor_tensor(top, top, vmax[:, :, 2:W + 2], ALU.max)
                elif step == 5 + has_halo:
                    ins = dve.tensor_tensor(vmax[:, :, 0:W].rearrange("p r (q w) -> p r q w", q=R),
                                            top.rearrange("p r (w q) -> p r q w", q=R),
                                            raw[:, k * R + 1:(k + 1) * R + 1, :].rearrange("p r (w q) -> p r q w", q=R),
                                            ALU.add)
                else:
                    return
                ins.then_inc(dil, 1)

            def make_g1(b, c):
                at = (c + 2) % NC
                dve.wait_ge(proj_filled, used(b, "center", c))
                dve.wait_ge(base_done, chunk(b, c + 1))
                normed(X1, g1[:, :], x1[:, at * T:(at + 1) * T]).then_inc(g1_done, 1)

            def pad(b, n):
                normed(Z0 + n, padded[:, 1:NB + 1, 1:W + 1].rearrange("p g (w q) -> p g q w", q=R),
                       z[:, :].rearrange("p (g q w) -> p g q w", g=NB, q=R)).then_inc(padded_done, 1)

            def add_conv(b, use):
                _, n, k = use
                dve.wait_ge(side_filled, used(b, *use))
                block_z = z[:, k * T:(k + 1) * T].rearrange("p (g q w) -> p g q w", g=CB, q=R)
                block_o = raw[:, 1 + CB * k:1 + CB * (k + 1), :].rearrange("p g (w q) -> p g q w", q=R)
                dve.tensor_tensor(block_o if n else block_z, side_ps[:, :].rearrange("p (g w q) -> p g q w", g=CB, q=R),
                                  block_z, ALU.add).then_inc(side_emptied, 1)

            def conv_stats(b, use):
                k = use[2]
                dve.wait_ge(side_emptied, read(b, *use))
                last = z_stats(Z1, k)
                if k == NC - 1:
                    last.then_inc(st, 1)

            def make_u(b, c, s):
                if s == 0:
                    dve.wait_ge(dtx_done, chunk(b, c, NH))
                dve.wait_ge(b_cast, state(b, c, s))
                dve.wait_ge(h_done, state(b, *behind(c, s, RING), NH))
                dve.tensor_tensor(u_in[:, s % RING], dtx[:, c % 2],
                                  b_ps[:, s % 2:s % 2 + 1, :].broadcast_to([P, NH, T]), ALU.mult).then_inc(u_made, 1)

            def scan(b, c, s, half):
                r = s % RING
                if half == 0:
                    dve.wait_ge(hc_done, state(b, *behind(c, s, RING)))
                    if (c or s >= RING) and (c < NC - 1 or s < RING):
                        dve.wait_ge(kept, kept_state(b, *behind(c, s, RING)))
                    dve.wait_ge(u_made, state(b, c, s))
                dve.wait_ge(a_made, state(b, c, s, NH) - (NH - 1 - half))
                start = carry[:, half, s:s + 1] if c else 0.0
                dve.tensor_tensor_scan(h[:, r, half], a[:, r, half], u_in[:, r, half], start,
                                       ALU.mult, ALU.add).then_inc(h_done, 1)

            def split_rest(b, c):
                dve.wait_ge(hi_done, chunk(b, c + 1))
                dve.tensor_tensor(rest[:, :], proj_ps[0:2 * S, :], parts[:, 0, :], ALU.subtract).then_inc(proj_emptied, 1)

            def split_lo(b, c):
                dve.wait_ge(mid_done, chunk(b, c + 1))
                dve.tensor_tensor(parts[:, 2, :], rest[:, :], parts[:, 1, :], ALU.subtract).then_inc(lo_done, 1)

            def add_skip(b, c):
                for half in range(NH):
                    dve.wait_ge(summed, state(b, *behind(c, 0, 1)))
                    dve.scalar_tensor_tensor(out=xc[:, (c + 1) % 2, half], in0=xc[:, (c + 1) % 2, half],
                                             scalar=d_skip[:, half:half + 1], in1=y_ps[:, half],
                                             op0=ALU.mult, op1=ALU.add).then_inc(skip_done, 1)

            def gate(b, c):
                dve.wait_ge(skip_done, chunk(b, c, NH))
                dve.tensor_tensor(xc[:, (c + 1) % 2], xc[:, (c + 1) % 2], zs[:, (c + 1) % 2],
                                  ALU.mult).then_inc(gated, 1)

            def residual(b, use):
                c = use[1]
                dve.wait_ge(side_filled, used(b, *use))
                dve.tensor_tensor(x2[:, (c + 1) % 2], x2[:, (c + 1) % 2], side_ps[:, :],
                                  ALU.add).then_inc(side_emptied, 1)

            dve.wait_ge(raw_in, 3 * 16)
            for k in range(NC):
                last = raw_stats(k)
            last.then_inc(st, 1)
            dve.sem_inc(proj_emptied, 1)
            dve.sem_inc(side_emptied, 1)
            group_local(0, "raw_first")
            group_deviation(0, "raw_first")
            group_shift(0, "raw_first")
            halo_scales(0)
            for k in range(BANDS):
                for step in range(len(DIL_SLOTS)):
                    dilate(0, k, step)
            dve.wait_ge(x1_in, C * 16)
            for k in range(NC):
                last = x1_stats(k)
            last.then_inc(st, 1)
            group_local(0, "x1_first")
            group_deviation(0, "x1_first")
            group_shift(0, "x1_first")
            normed(X1, g1[:, :], x1[:, 0:T]).then_inc(g1_done, 1)
            make_g1(0, -1)
            split_rest(0, -1)
            split_lo(0, -1)
            start_ahead(dve, u_made)
            start_ahead(dve, h_done, n=NH)
            with dve.Fori(0, B) as b:
                make_u(b, 0, 0)
                for c in range(NC):
                    for s in range(S):
                        scan(b, c, s, 0)
                        if s == SKIP:
                            add_skip(b, c)
                        if s + 1 < S or c + 1 < NC:
                            make_u(b, *behind(c, s, -1))
                        scan(b, c, s, 1)
                        if s == GATE:
                            gate(b, c)
                        if s == OUT:
                            residual(b, ("out", c))
                        if s == SPLIT_REST:
                            split_rest(b, c)
                        if s == SPLIT_LO:
                            split_lo(b, c)
                        if c == RAW_STATS[0] and 0 <= s - RAW_STATS[1] < NC:
                            if s == RAW_STATS[1]:
                                dve.wait_ge(raw_in, (b + 2) * 3 * 16)
                            raw_stats(s - RAW_STATS[1])
                        if c == Z_STATS[0] and 0 <= s - Z_STATS[1] < NC:
                            if s == Z_STATS[1]:
                                dve.wait_ge(z_in, (b + 1) * BANDS * 16)
                            last = z_stats(Z0, s - Z_STATS[1])
                            if s - Z_STATS[1] == NC - 1:
                                last.then_inc(st, 1)
                                group_local(b, "joint")
                        if c == X1_STATS[0] and 0 <= s - X1_STATS[1] < NC:
                            if s == X1_STATS[1]:
                                dve.wait_ge(x1_in, (b + 2) * C * 16)
                            last = x1_stats(s - X1_STATS[1])
                            if s - X1_STATS[1] == NC - 1:
                                last.then_inc(st, 1)
                                group_local(b, "x1")
                        for name in MEAN_AT:
                            if MEAN_AT[name] == (c, s - 1):
                                group_deviation(b, name)
                            if VAR_AT[name] == (c, s - 2):
                                group_shift(b, name)
                                if name == "joint":
                                    halo_scales(b + 1)
                        for n in range(2):
                            if PADDED_AT[n] == (c, s):
                                pad(b, n)
                        if 1 <= c <= BANDS and s in DIL_SLOTS:
                            dilate(b + 1, c - 1, DIL_SLOTS.index(s))
                        for (n, k), states in CONV_AT.items():
                            if states[-1] == c * S + s:
                                add_conv(b, ("conv", n, k))
                            if n == 0 and states[-1] + 1 == c * S + s:
                                conv_stats(b, ("conv", n, k))
                                if k == NC - 1:
                                    group_local(b, "z1")
                        if s == NEXT_G1:
                            make_g1(b, c)
            add_skip(B, 0)
            gate(B, 0)
            residual(B, ("out_last", 0))
            dve.wait_ge(z_in, (B + 1) * BANDS * 16)
            for k in range(NC):
                last = z_stats(Z0, k)
            last.then_inc(st, 1)
            for n, name in enumerate(("z0_last", "z1_last")):
                group_local(B, name)
                group_deviation(B, name)
                group_shift(B, name)
                pad(B, n)
                for k in range(NC):
                    add_conv(B, ("conv_last", n, k))
                    if n == 0:
                        conv_stats(B, ("conv_last", n, k))


def tables():
    import numpy as np

    group = np.kron(np.eye(4), np.full((32, 32), 1 / 32))
    in_comb = (np.arange(P) % (C * R)) // (2 * R)
    group_z = (in_comb[:, None] == in_comb[None, :]) / 32
    select = np.tile(np.kron(np.eye(S), np.ones((1, P))), (3, 1))
    band = np.arange(P) % NB
    top, bottom = (band > 0).astype(np.float64), (band < NB - 1).astype(np.float64)
    halo = np.stack([top, BORDER * (1 - top), bottom, BORDER * (1 - bottom)], axis=1)
    row = np.arange(P) // (C * R) * R + np.arange(P) % R
    taps = np.stack([row[:, None] == np.arange(BAND)[None, :] + kh - 1 for kh in range(3)], axis=1)
    said = {
        "center": np.eye(P) - 1 / P, "mean": np.full((P, P), 1 / P), "ident": np.eye(P), "group": group,
        "group_z": group_z, "halo": halo, "select": select, "taps": taps.reshape(P, 3 * BAND),
    }
    return {k: v.astype(np.float32) for k, v in said.items()}


def kernel(x, L1_conv_ln_gamma, L1_conv_ln_beta, L1_conv_in_proj_w, L1_conv_conv_w, L1_conv_conv_b,
           L1_conv_x_proj_w, L1_conv_dt_proj_w, L1_conv_dt_proj_b, L1_conv_A_log, L1_conv_D,
           L1_conv_out_proj_w, L2_conv_weight, L2_conv_bias, L3_conv_weight, L3_conv_bias):
    import numpy as np
    import concourse.bacc as bacc
    from concourse.bass_utils import run_bass_kernel_spmd

    def column(a):
        return np.asarray(a).reshape(-1, 1)

    xp = np.asarray(L1_conv_x_proj_w)
    scan_w = {
        "in_x_t": np.asarray(L1_conv_in_proj_w)[:DI].T, "in_z_t": np.asarray(L1_conv_in_proj_w)[DI:].T,
        "x_proj_t": np.concatenate([xp[DTR:], xp[:DTR]]).T,
        "out_proj_t": np.asarray(L1_conv_out_proj_w).T, "dt_proj_t": np.asarray(L1_conv_dt_proj_w).T,
        "conv_w_t": np.asarray(L1_conv_conv_w).reshape(DI, TAPS).T, "conv_b": column(L1_conv_conv_b),
        "dt_b": column(L1_conv_dt_proj_b), "d": column(L1_conv_D), "a_log": np.asarray(L1_conv_A_log),
        "gamma": column(L1_conv_ln_gamma), "beta": column(L1_conv_ln_beta),
    }
    convs = {}
    for n, (w, bias) in enumerate(((L2_conv_weight, L2_conv_bias), (L3_conv_weight, L3_conv_bias))):
        w = np.asarray(w)
        by_tap = w.transpose(1, 2, 3, 0).reshape(C, 9 * C)
        convs[f"main{n}"] = np.tile(np.repeat(by_tap, R, axis=0), (BANDS, 1))
        convs[f"above{n}"] = w[:, :, 0, :].transpose(2, 1, 0).reshape(3 * C, C)
        convs[f"below{n}"] = w[:, :, 2, :].transpose(2, 1, 0).reshape(3 * C, C)
        convs[f"bias{n}"] = np.tile(np.repeat(np.asarray(bias), R), BANDS).reshape(1, P)

    nc = bacc.Bacc("TRN2", target_bir_lowering=False, num_devices=1)
    arrays = {}

    def give(name, a):
        a = np.ascontiguousarray(a)
        arrays[name] = a
        return nc.dram_tensor(name, a.shape, mybir.dt.from_np(a.dtype), kind="ExternalInput").ap()

    x_in = give("x", x)
    scan_in = {k: give(f"mamba_{k}", v) for k, v in scan_w.items()}
    conv_in = {k: give(f"conv_{k}", v) for k, v in convs.items()}
    table_in = {k: give(f"table_{k}", v) for k, v in tables().items()}
    out = nc.dram_tensor("out", (B, C, H, W), F32, kind="ExternalOutput").ap()
    build(nc, x_in, scan_in, conv_in, table_in, out)
    return run_bass_kernel_spmd(nc, [arrays], core_ids=[0]).results[0]["out"]
```
